# Optimizing a Trainium2 kernel written in Bass

```python
import numpy as np
import jax
import jax.numpy as jnp

def _softmax(x, axis=-1):
    return jax.nn.softmax(x, axis=axis)

def _gelu(x):
    return jax.nn.gelu(x, approximate=True)

def _silu(x):
    return jax.nn.silu(x)

def _sigmoid(x):
    return jax.nn.sigmoid(x)

def _layernorm(x, axis=-1, eps=1e-05):
    m = jnp.mean(x, axis=axis, keepdims=True)
    v = jnp.var(x, axis=axis, keepdims=True)
    return (x - m) / jnp.sqrt(v + eps)

def _scatter_add(tgt, idx, src, axis=0):
    return tgt.at[idx].add(src)

def _segment_sum(src, seg, n):
    return jax.ops.segment_sum(src, seg, n)
kernel_name = 'mk_xattn_ffn_d1_seqx_r8_1f67dd'

def setup_inputs(seed: int=0):
    np.random.seed(seed)
    _w = jnp.asarray

    def _rec_inputs():
        import jax
        import jax.numpy as jnp
        _rk = jax.random.key(seed)
        x = -0.0005857 + 0.9999 * jax.random.normal(jax.random.fold_in(_rk, 1), (64, 64, 128), jnp.float32)
        _lenS = 64 - jax.random.randint(jax.random.fold_in(_rk, 7), (64,), 0, max(1, 64 // 4) + 1, jnp.int32)
        _lenS2 = 64 - jax.random.randint(jax.random.fold_in(_rk, 8), (64,), 0, max(1, 64 // 4) + 1, jnp.int32)
        _ctx_1024P = jax.random.normal(jax.random.fold_in(_rk, 11), (64, 16, 128), jnp.float32)
        _ctx_1024c = jax.random.dirichlet(jax.random.fold_in(_rk, 511), 0.3 * jnp.ones((16,), jnp.float32), (64, 64))
        _ctx_1024t = jnp.einsum('bsk,bkd->bsd', _ctx_1024c, _ctx_1024P)
        _ctx_1024t = _ctx_1024t * jax.lax.rsqrt(jnp.mean(jnp.square(_ctx_1024t)) + 1e-12) * 0.953939
        ctx_1024 = -0.000264403 + 1.00002 * (_ctx_1024t + 0.3 * jax.random.normal(jax.random.fold_in(_rk, 611), (64, 64, 128), jnp.float32))
        return (x, ctx_1024)
    x, ctx_1024 = _rec_inputs()

    def _L0_xattn_setup():
        import jax, jax.numpy as jnp
        import numpy as np
        D_MODEL = 128
        N_HEADS = 16
        D_K = D_MODEL // N_HEADS
        key = jax.random.key(seed)
        ks = jax.random.split(key, 12)
        B, S, D = (2, 256, D_MODEL)
        lim = 1.0 / np.sqrt(D)

        def lin(k):
            kw, kb = jax.random.split(k)
            W = jax.random.uniform(kw, (D, D), jnp.float32, -lim, lim)
            b = jax.random.uniform(kb, (D,), jnp.float32, -lim, lim)
            return (W, b)
        wq, bq = lin(ks[0])
        wk, bk = lin(ks[1])
        wv, bv = lin(ks[2])
        wo, bo = lin(ks[3])
        return {'query': jax.random.normal(ks[4], (B, S, D), jnp.float32), 'key': jax.random.normal(ks[5], (B, S, D), jnp.float32), 'value': jax.random.normal(ks[6], (B, S, D), jnp.float32), 'wq': wq, 'bq': bq, 'wk': wk, 'bk': bk, 'wv': wv, 'bv': bv, 'wo': wo, 'bo': bo, 'time_decay': jnp.float32(0.1)}
    _L0_xattn_all = _L0_xattn_setup()
    _L0_xattn_in = {k: v for k, v in _L0_xattn_all.items() if k in ('wq', 'bq', 'wk', 'bk', 'wv', 'bv', 'wo', 'bo', 'time_decay')}
    del _L0_xattn_all

    def _L0_ffn_setup():
        import jax, jax.numpy as jnp
        import numpy as np
        S, B, D, H, E, K, F = (128, 4, 128, 16, 8, 2, 512)

        def _ln(x, g, b, eps=1e-05):
            mu = jnp.mean(x, axis=-1, keepdims=True)
            var = jnp.mean((x - mu) ** 2, axis=-1, keepdims=True)
            return (x - mu) * jax.lax.rsqrt(var + eps) * g + b
        key = jax.random.key(seed)
        ks = jax.random.split(key, 8)
        s = 0.02
        return {'src': jax.random.normal(ks[0], (S, B, D), jnp.float32), 'in_proj_w': jax.random.normal(ks[1], (3 * D, D), jnp.float32) * s, 'in_proj_b': jnp.zeros((3 * D,), jnp.float32), 'out_w': jax.random.normal(ks[2], (D, D), jnp.float32) * s, 'out_b': jnp.zeros((D,), jnp.float32), 'gate_w': jax.random.normal(ks[3], (E, D), jnp.float32) * s, 'gate_b': jnp.zeros((E,), jnp.float32), 'w1': jax.random.normal(ks[4], (E, F, D), jnp.float32) * s, 'b1': jnp.zeros((E, F), jnp.float32), 'w2': jax.random.normal(ks[5], (E, D, F), jnp.float32) * s, 'b2': jnp.zeros((E, D), jnp.float32), 'ln1_g': jnp.ones((D,), jnp.float32), 'ln1_b': jnp.zeros((D,), jnp.float32), 'ln2_g': jnp.ones((D,), jnp.float32), 'ln2_b': jnp.zeros((D,), jnp.float32)}
    _L0_ffn_all = _L0_ffn_setup()
    _L0_ffn_in = {k: v for k, v in _L0_ffn_all.items() if k in ('in_proj_w', 'in_proj_b', 'out_w', 'out_b', 'gate_w', 'gate_b', 'w1', 'b1', 'w2', 'b2', 'ln1_g', 'ln1_b', 'ln2_g', 'ln2_b')}
    del _L0_ffn_all
    return {'x': x, 'ctx_1024': ctx_1024, 'L0_xattn_wq': _L0_xattn_in['wq'], 'L0_xattn_bq': _L0_xattn_in['bq'], 'L0_xattn_wk': _L0_xattn_in['wk'], 'L0_xattn_bk': _L0_xattn_in['bk'], 'L0_xattn_wv': _L0_xattn_in['wv'], 'L0_xattn_bv': _L0_xattn_in['bv'], 'L0_xattn_wo': _L0_xattn_in['wo'], 'L0_xattn_bo': _L0_xattn_in['bo'], 'L0_xattn_time_decay': _L0_xattn_in['time_decay'], 'L0_ffn_in_proj_w': _L0_ffn_in['in_proj_w'], 'L0_ffn_in_proj_b': _L0_ffn_in['in_proj_b'], 'L0_ffn_out_w': _L0_ffn_in['out_w'], 'L0_ffn_out_b': _L0_ffn_in['out_b'], 'L0_ffn_gate_w': _L0_ffn_in['gate_w'], 'L0_ffn_gate_b': _L0_ffn_in['gate_b'], 'L0_ffn_w1': _L0_ffn_in['w1'], 'L0_ffn_b1': _L0_ffn_in['b1'], 'L0_ffn_w2': _L0_ffn_in['w2'], 'L0_ffn_b2': _L0_ffn_in['b2'], 'L0_ffn_ln1_g': _L0_ffn_in['ln1_g'], 'L0_ffn_ln1_b': _L0_ffn_in['ln1_b'], 'L0_ffn_ln2_g': _L0_ffn_in['ln2_g'], 'L0_ffn_ln2_b': _L0_ffn_in['ln2_b']}

def reference(x, ctx_1024, L0_xattn_wq, L0_xattn_bq, L0_xattn_wk, L0_xattn_bk, L0_xattn_wv, L0_xattn_bv, L0_xattn_wo, L0_xattn_bo, L0_xattn_time_decay, L0_ffn_in_proj_w, L0_ffn_in_proj_b, L0_ffn_out_w, L0_ffn_out_b, L0_ffn_gate_w, L0_ffn_gate_b, L0_ffn_w1, L0_ffn_b1, L0_ffn_w2, L0_ffn_b2, L0_ffn_ln1_g, L0_ffn_ln1_b, L0_ffn_ln2_g, L0_ffn_ln2_b):
    import jax
    import jax.numpy as jnp

    def _L0_xattn_ref(query, key, value, wq, bq, wk, bk, wv, bv, wo, bo, time_decay):
        import jax, jax.numpy as jnp
        import numpy as np
        D_MODEL = 128
        N_HEADS = 16
        D_K = D_MODEL // N_HEADS
        B, S, D = query.shape
        H, Dk = (N_HEADS, D_K)

        def proj(x, W, b):
            y = jnp.einsum('bsd,ed->bse', x, W) + b
            return y.reshape(B, S, H, Dk).transpose(0, 2, 1, 3)
        Q = proj(query, wq, bq)
        K = proj(key, wk, bk)
        V = proj(value, wv, bv)
        scores = jnp.einsum('bhqd,bhkd->bhqk', Q, K) / jnp.sqrt(jnp.float32(Dk))
        pos = jnp.arange(S, dtype=jnp.float32)
        decay = -time_decay * jnp.abs(pos[:, None] - pos[None, :])
        scores = scores + decay[None, None, :, :]
        attn = jax.nn.softmax(scores, axis=-1)
        ctx = jnp.einsum('bhqk,bhkd->bhqd', attn, V)
        ctx = ctx.transpose(0, 2, 1, 3).reshape(B, S, D)
        out = jnp.einsum('bsd,ed->bse', ctx, wo) + bo
        return out

    def _L0_ffn_ref(src, in_proj_w, in_proj_b, out_w, out_b, gate_w, gate_b, w1, b1, w2, b2, ln1_g, ln1_b, ln2_g, ln2_b):
        import jax, jax.numpy as jnp
        import numpy as np
        S, B, D, H, E, K, F = (128, 4, 128, 16, 8, 2, 512)

        def _ln(x, g, b, eps=1e-05):
            mu = jnp.mean(x, axis=-1, keepdims=True)
            var = jnp.mean((x - mu) ** 2, axis=-1, keepdims=True)
            return (x - mu) * jax.lax.rsqrt(var + eps) * g + b
        s_len, bsz, d = src.shape
        dh = d // H
        qkv = src @ in_proj_w.T + in_proj_b
        q, k, v = jnp.split(qkv, 3, axis=-1)
        q = q.reshape(s_len, bsz, H, dh)
        k = k.reshape(s_len, bsz, H, dh)
        v = v.reshape(s_len, bsz, H, dh)
        scale = dh ** (-0.5)
        scores = jnp.einsum('sbhd,tbhd->bhst', q, k) * scale
        attn = jax.nn.softmax(scores, axis=-1)
        ctx = jnp.einsum('bhst,tbhd->sbhd', attn, v).reshape(s_len, bsz, d)
        attn_out = ctx @ out_w.T + out_b
        x = _ln(src + attn_out, ln1_g, ln1_b)
        tok = x.reshape(-1, d)
        n_tok = tok.shape[0]
        logits = tok @ gate_w.T + gate_b
        probs = jax.nn.softmax(logits, axis=-1)
        topv, topi = jax.lax.top_k(probs, K)
        topv = topv / jnp.sum(topv, axis=-1, keepdims=True)
        combine = jnp.zeros_like(probs).at[jnp.arange(n_tok)[:, None], topi].set(topv)
        moe_out = jnp.zeros_like(tok)
        for e in range(E):
            h = jax.nn.relu(tok @ w1[e].T + b1[e]) @ w2[e].T + b2[e]
            moe_out = moe_out + combine[:, e:e + 1] * h
        moe_out = moe_out.reshape(s_len, bsz, d)
        return _ln(x + moe_out, ln2_g, ln2_b)
    x = x + _L0_xattn_ref(_layernorm(x, axis=-1), ctx_1024, ctx_1024, L0_xattn_wq, L0_xattn_bq, L0_xattn_wk, L0_xattn_bk, L0_xattn_wv, L0_xattn_bv, L0_xattn_wo, L0_xattn_bo, L0_xattn_time_decay)
    x = x + _L0_ffn_ref(_layernorm(x, axis=-1), L0_ffn_in_proj_w, L0_ffn_in_proj_b, L0_ffn_out_w, L0_ffn_out_b, L0_ffn_gate_w, L0_ffn_gate_b, L0_ffn_w1, L0_ffn_b1, L0_ffn_w2, L0_ffn_b2, L0_ffn_ln1_g, L0_ffn_ln1_b, L0_ffn_ln2_g, L0_ffn_ln2_b)
    return x

_drawn_inputs = setup_inputs


def setup_inputs(seed=0):
    import zlib

    import numpy as np

    out = dict(_drawn_inputs(seed))
    spreads = {'L0_ffn_in_proj_b': (0.0, 0.571),
     'L0_ffn_out_b': (0.0, 0.1),
     'L0_ffn_gate_b': (0.0, 0.1),
     'L0_ffn_b1': (0.0, 0.798),
     'L0_ffn_b2': (0.0, 0.1),
     'L0_ffn_ln1_g': (1.0, 0.2),
     'L0_ffn_ln1_b': (0.0, 0.1),
     'L0_ffn_ln2_g': (1.0, 0.2),
     'L0_ffn_ln2_b': (0.0, 0.1)}
    factors = {'L0_xattn_bq': 8.0, 'L0_xattn_bk': 8.0, 'L0_ffn_in_proj_w': 8.0, 'L0_ffn_out_w': 4.603}
    for name, (base, spread) in spreads.items():
        noise = np.random.default_rng([zlib.crc32(name.encode()), seed]).standard_normal(out[name].shape)
        drawn = base * np.exp(spread * noise) if base else spread * noise
        out[name] = jnp.asarray(drawn.astype(out[name].dtype))
    for name, factor in factors.items():
        out[name] = (out[name] * factor).astype(out[name].dtype)
    return out
```

```python
import concourse.bass as bass
from concourse import mybir
from contextlib import ExitStack

FP32 = mybir.dt.float32
FP32R = mybir.dt.float32r
UINT32 = mybir.dt.uint32
INT32 = mybir.dt.int32
ALU = mybir.AluOpType
ACT = mybir.ActivationFunctionType
AX = mybir.AxisListType

B, S, D = 64, 64, 128
H = 16
DH = D // H
P = 128
NT = B * S // P
G4 = 4
VW = 2 * (DH + 1)
EPS = 1e-5
ROOT = float(DH) ** 0.5
N_EXP, F = 8, 512
FC = F // P
TOP = 2
NM = (TOP * B * S + N_EXP * (P - 1)) // P
NM += -NM % 4
FAR = 3.0e38


def build(nc, t, out, scratch, packed, expert_out):
    ctx = ExitStack()
    with ctx:
        def sb(name, shape, dt=FP32):
            return ctx.enter_context(nc.sbuf_tensor(name, shape, dt))

        def ps(name, cols):
            return ctx.enter_context(nc.psum_tensor(name, [P, cols], FP32))

        def sem(name):
            return ctx.enter_context(nc.semaphore(name))

        ident = sb("ident", [P, P])
        dist = sb("dist", [P, S])
        mask_q = sb("mask_q", [P, G4])
        mask_k = sb("mask_k", [P, G4])
        neg_half = sb("neg_half", [P, 1])
        decay = sb("decay", [P, S])
        td = sb("td", [P, 1])
        w_rows = sb("w_rows", [P, 8, D])
        w_t = sb("w_t", [P, 8, D])
        gate_rows = sb("gate_rows", [N_EXP, D])
        gate_t = sb("gate_t", [P, N_EXP])
        bias_qk = sb("bias_qk", [P, 2, 2])
        bias_v = sb("bias_v", [P, 2])
        bias_v_wide = sb("bias_v_wide", [P, 2, P])
        bias_g = sb("bias_g", [P, N_EXP])
        bias_o = sb("bias_o", [P, 2, D])
        row_add = sb("row_add", [P, 2, D])
        ln1 = sb("ln1", [P, 2, D])
        ln2 = sb("ln2", [P, 2, D])
        w_hi = [sb(f"w{n}_hi", [P, N_EXP, F], FP32R) for n in (1, 2)]
        w_lo = [sb(f"w{n}_lo", [P, N_EXP, F], FP32R) for n in (1, 2)]
        b1_wide = sb("b1_wide", [P, N_EXP, F])
        b2_wide = sb("b2_wide", [P, N_EXP, D])
        zero_tile = sb("zero_tile", [P, D])
        earlier = sb("earlier", [P, P])
        ones = sb("ones", [P, P])
        rank8 = sb("rank8", [P, N_EXP])
        steps128 = sb("steps128", [P, NT])
        tile_no = sb("tile_no", [P, NM])
        x_all = sb("x_all", [P, NT, D])
        src_all = sb("src_all", [P, NT, D])
        ctx_in = sb("ctx_in", [P, 4, D])
        xn = sb("xn", [P, 2, D])
        xct = sb("xct", [P, 2, 2, D])
        qm = sb("qm", [P, 2, G4, P])
        kx = sb("kx", [P, 2, G4, P])
        vb = sb("vb", [P, 4, 2, H // 2, 2, DH + 1])
        prob = sb("prob", [P, 2, H, S])
        probt = sb("probt", [P, 2, H // 2, P])
        neg_max = sb("neg_max", [P, 2, H])
        inv_sum = sb("inv_sum", [P, 2, H])
        o_sb = sb("o_sb", [P, 2, D])
        ot_sb = sb("ot_sb", [P, 2, D])
        stats_a = sb("stats_a", [P, 2, 6])
        mv_a = sb("mv_a", [P, 2, 2])
        rs_a = sb("rs_a", [P, 2, 2])
        stats_b = sb("stats_b", [P, 2, 6])
        mv_b = sb("mv_b", [P, 2, 2])
        rs_b = sb("rs_b", [P, 2, 2])
        res = sb("res", [P, 4, 2, D])
        tok_t = sb("tok_t", [P, 2, P])
        logit = sb("logit", [P, NT, N_EXP])
        with ExitStack() as early:
            w1_rows = early.enter_context(nc.sbuf_tensor("w1_rows", [P, N_EXP * FC, D], FP32))
            w2_rows = early.enter_context(nc.sbuf_tensor("w2_rows", [P, N_EXP, F], FP32))
        best = sb("best", [P, TOP, NT])
        pick = sb("pick", [P, TOP, NT, N_EXP])
        r_key = sb("r_key", [P, NT, N_EXP])
        r_top = sb("r_top", [P, NT])
        rest = sb("rest", [P, NT, N_EXP])
        both = sb("both", [P, NT, N_EXP])
        scan = sb("scan", [P, 2, NT, N_EXP])
        place = sb("place", [P, NT, N_EXP])
        slot_f = sb("slot_f", [P, TOP, NT])
        slot_u = sb("slot_u", [P, TOP, NT], UINT32)
        share = sb("share", [P, TOP, NT])
        r_exp = sb("r_exp", [P, NT])
        r_sum = sb("r_sum", [P, NT])
        full = sb("full", [P, N_EXP, NT])
        tiles_of = sb("tiles_of", [P, N_EXP])
        tiles_to = sb("tiles_to", [P, 2, N_EXP])
        starts = sb("starts", [P, N_EXP])
        past = sb("past", [P, NM, N_EXP])
        expert_f = sb("expert_f", [P, NM])
        expert_of = sb("expert_of", [P, NM], INT32)
        tok_slot = sb("tok_slot", [P, 4, D])
        idx_slot = sb("idx_slot", [P, 4, TOP], UINT32)
        xs = sb("xs", [P, 4, D])
        x_hi = sb("x_hi", [P, 2, P], FP32R)
        x_lo = sb("x_lo", [P, 2, P], FP32R)
        h_hi = sb("h_hi", [P, 2, F], FP32R)
        h_lo = sb("h_lo", [P, 2, F], FP32R)

        flat_a = prob[:, :, :, :].rearrange("p s h k -> p (s h k)")
        flat_b = probt[:, :, :, :].rearrange("p s h q -> p (s h q)")
        got = flat_a[:, 0:8 * D].rearrange("p (s c d) -> p s c d", s=4, c=TOP)
        x1_in = flat_a[:, 8 * D:12 * D].rearrange("p (s d) -> p s d", s=4)
        z_sb = flat_a[:, 12 * D:16 * D].rearrange("p (s d) -> p s d", s=4)
        h_sb = flat_b[:, 0:2 * F].rearrange("p (s f) -> p s f", s=2)
        y_sb = flat_b[:, 8 * D:12 * D].rearrange("p (s d) -> p s d", s=4)
        o_out = flat_b[:, 12 * D:16 * D].rearrange("p (s d) -> p s d", s=4)

        ps_in = ps("ps_in", 512)
        ps_qk = ps("ps_qk", 512)
        ps_s = ps("ps_s", 1024)
        ps_pt = ps("ps_pt", 1024)
        ps_o = ps("ps_o", 512)
        ps_y = ps("ps_y", 512)

        const2_in = sem("const2_in")
        weights_in, const_in, x_in0, x_in1 = sem("weights_in"), sem("const_in"), sem("x_in0"), sem("x_in1")
        src_in = [sem(f"src_in{n}") for n in range(4)]
        zeroed, w_transposed, w_ready, row_done, prep = sem("zeroed"), sem("w_transposed"), sem("w_ready"), sem("row_done"), sem("prep")
        row_ready = sem("row_ready")
        ctx_ready = [sem(f"ctx_ready{n}") for n in range(4)]
        stored = [sem(f"stored{n}") for n in range(4)]
        names = ("x_stats x_mv x_var x_rstd xn_ready residual_ready in_done in_ready proj_done qk_ready "
                 "v_ready scores_done scores_read max_ready shifted probs_ready pt_done pt_ready pv_done "
                 "inv_ready o_ready ot_done ot_ready y_done y_read y_stats y_mv y_var y_rstd y_norm y_gain "
                 "y_ready tok_done tok_ready logits_done logits_read").split()
        att = {n: sem(n) for n in names}
        names = ("w_turned w_hi_ready w_lo_ready counted route_exp route "
                 "xt_done xhi_ready xlo_ready h_done hb_ready ht_done hhi_ready hlo_ready yy_done yo_ready "
                 "tok_copied idx_copied z_part z_ready z_stats z_mv z_var z_rstd z_norm z_gain o_done x1_added tok_kept").split()
        moe = {n: sem(n) for n in names}
        expert_rows_in, blanked, zero_ready = sem("expert_rows_in"), sem("blanked"), sem("zero_ready")
        packed_out = [sem(f"packed_out{n}") for n in range(4)]
        xs_in = [sem(f"xs_in{n}") for n in range(4)]
        y_out = [sem(f"y_out{n}") for n in range(4)]
        got_in = [sem(f"got_in{n}") for n in range(4)]
        x1_read = [sem(f"x1_read{n}") for n in range(4)]
        out_done = [sem(f"out_done{n}") for n in range(4)]
        dve_passed, pool_passed = sem("dve_passed"), sem("pool_passed")

        block = ctx.enter_context(nc.Block())

        def run_attention(eng, phase, step):
            first = phase * NT
            for n in range(-4, 8):
                step(first + n, first + n, phase, False)
            with eng.Fori(2, NT // 4 - 1) as i:
                for u in range(4):
                    step(i * 4 + (first + u), first + 8 + u, phase, True)
            for n in range(NT - 4, NT + 4):
                step(first + n, first + n, phase, False)

        def run_tiles(eng, count, behind, ahead, step):
            for n in range(-ahead, 8):
                step(n, n, False)
            with eng.Fori(2, count // 4 - 1) as i:
                for u in range(4):
                    step(i * 4 + u, 8 + u, True)
            for n in range(count - 4, count + behind):
                step(n, n, False)

        def wait_apart(eng, passed, semaphore, value):
            eng.wait_ge(semaphore, value)
            eng.sem_inc(passed, 1)

        def live(k, phase, looping):
            return looping or 0 <= k - phase * NT < NT

        @block.sync
        def _(sp):
            sp.dma_start(w_rows[:, 0, :], t["wq"]).then_inc(weights_in, 16)
            sp.dma_start(w_rows[:, 1, :], t["wk"]).then_inc(weights_in, 16)
            sp.dma_start(w_rows[:, 2, :], t["wv"]).then_inc(weights_in, 16)
            sp.dma_start(w_rows[:, 3, :], t["wo"]).then_inc(weights_in, 16)
            sp.dma_start(w_rows[:, 4:7, :], t["in_proj_w"].rearrange("(n e) d -> e n d", e=D)).then_inc(weights_in, 16)
            sp.dma_start(w_rows[:, 7, :], t["out_w"]).then_inc(weights_in, 16)
            sp.dma_start(gate_rows[:, :], t["gate_w"]).then_inc(weights_in, 16)
            x_v = t["x"].rearrange("b s d -> (b s) d").rearrange("(n p) d -> p n d", p=P)
            c_v = t["ctx"].rearrange("b s d -> (b s) d")
            sp.dma_start(x_all[:, 8:NT, :], x_v[:, 8:NT, :]).then_inc(x_in1, 16)
            sp.dma_start(w1_rows[:, :, :], t["w1"].rearrange("e (c f) d -> f (e c) d", f=P)).then_inc(expert_rows_in, 16)
            sp.dma_start(w2_rows[:, :, :], t["w2"].rearrange("e d f -> d e f")).then_inc(expert_rows_in, 16)
            sp.wait_ge(zero_ready, 1)
            sp.dma_start(packed.rearrange("(n p) d -> p n d", p=P), zero_tile[:, :].unsqueeze(1).broadcast_to([P, NM, D])).then_inc(blanked, 16)

            def step(t_, k, phase, looping):
                p, kp = t_ + 4, k + 4
                if phase == 0 and live(kp, phase, looping):
                    if kp >= 4:
                        sp.wait_ge(att["in_done"], p - 3)
                    sp.dma_start(ctx_in[:, kp % 4, :], c_v[bass.ds(p * P, P), :]).then_inc(ctx_ready[kp % 4], 16)
                p, kp = t_ - 2, k - 2
                if phase == 0 and live(kp, phase, looping):
                    sp.wait_ge(att["y_ready"], p + 1)
                    sp.dma_start(scratch[bass.ds(p * P, P), :, :], res[:, kp % 4, :, :]).then_inc(stored[kp % 4], 16)

            run_attention(sp, 0, step)
            for n in range(4):
                sp.wait_ge(stored[n], 16 * NT // 4)
            s_v = scratch.rearrange("(i r c) a d -> c i r a d", i=B, c=2)
            for n in range(4):
                for c in range(2):
                    sp.dma_start(src_all[c * 64:c * 64 + 64, 8 * n:8 * n + 8, :], s_v[c, :, 8 * n:8 * n + 8, 1, :]).then_inc(src_in[n], 16)

            for n in range(4):
                sp.wait_ge(packed_out[n], 2 * 16 * NT // 4)

            def expert_step(t_, k, looping):
                p, kp = t_ + 3, k + 3
                if looping or 0 <= kp < NM:
                    if kp >= 4:
                        sp.wait_ge(moe["xt_done"], p - 3)
                    sp.dma_start(xs[:, kp % 4, :], packed[bass.ds(p * P, P), :]).then_inc(xs_in[kp % 4], 16)
                p, kp = t_ - 2, k - 2
                if looping or 0 <= kp < NM:
                    sp.wait_ge(moe["yo_ready"], p + 1)
                    sp.dma_start(expert_out[bass.ds(p * P, P), :], y_sb[:, kp % 4, :]).then_inc(y_out[kp % 4], 16)

            run_tiles(sp, NM, 2, 3, expert_step)

            x1_v = scratch.rearrange("(i r c) a d -> c r i a d", i=B, c=2)
            out_v = out.rearrange("i (r c) d -> c r i d", c=2)

            def combine_step(t_, k, looping):
                p, kp = t_ + 3, k + 3
                if looping or 0 <= kp < NT:
                    if kp >= 4:
                        sp.wait_ge(moe["o_done"], p - 3)
                    for c in range(2):
                        sp.dma_start(x1_in[64 * c:64 * c + 64, kp % 4, :], x1_v[c, p, :, 0, :]).then_inc(x1_read[kp % 4], 16)
                p, kp = t_ - 1, k - 1
                if looping or 0 <= kp < NT:
                    sp.wait_ge(moe["o_done"], p + 1)
                    for c in range(2):
                        sp.dma_start(out_v[c, p, :, :], o_out[64 * c:64 * c + 64, kp % 4, :]).then_inc(out_done[kp % 4], 16)

            run_tiles(sp, NT, 1, 3, combine_step)
            for n in range(4):
                sp.wait_ge(out_done[n], 2 * 16 * NT // 4)

        @block.scalar
        def _(act):
            act.dma_start(x_all[:, 0:8, :], t["x"].rearrange("b s d -> (b s) d").rearrange("(n p) d -> p n d", p=P)[:, 0:8, :]).then_inc(x_in0, 16)
            act.dma_start(bias_g[:, :], t["gate_b"].unsqueeze(0).broadcast_to([P, N_EXP])).then_inc(const_in, 16)
            act.dma_start(ident[:, :], t["ident"]).then_inc(const_in, 16)
            act.dma_start(dist[:, :], t["dist"]).then_inc(const_in, 16)
            act.dma_start(mask_q[:, :], t["mask_q"]).then_inc(const_in, 16)
            act.dma_start(mask_k[:, :], t["mask_k"]).then_inc(const_in, 16)
            act.dma_start(td[:, :], t["time_decay"].broadcast_to([P, 1])).then_inc(const_in, 16)
            for n, a in enumerate((t["bq"], t["bk"], t["in_proj_b"][0:D], t["in_proj_b"][D:2 * D])):
                act.dma_start(bias_qk[:, n // 2, n % 2:n % 2 + 1], a.unsqueeze(1)).then_inc(const_in, 16)
            for n, a in enumerate((t["bv"], t["in_proj_b"][2 * D:3 * D])):
                act.dma_start(bias_v[:, n:n + 1], a.unsqueeze(1)).then_inc(const_in, 16)
            for n, a in enumerate((t["bo"], t["out_b"])):
                act.dma_start(bias_o[:, n, :], a.unsqueeze(0).broadcast_to([P, D])).then_inc(const_in, 16)
            for n, a in enumerate((t["ln1_g"], t["ln1_b"])):
                act.dma_start(ln1[:, n, :], a.unsqueeze(0).broadcast_to([P, D])).then_inc(const_in, 16)
            for n, a in enumerate((t["ln2_g"], t["ln2_b"])):
                act.dma_start(ln2[:, n, :], a.unsqueeze(0).broadcast_to([P, D])).then_inc(const2_in, 16)
            for a, name in ((earlier, "earlier"), (rank8, "rank8"), (steps128, "steps128"), (tile_no, "tile_no")):
                act.dma_start(a[:, :], t[name]).then_inc(const2_in, 16)
            act.dma_start(b1_wide[:, :, :], t["b1"].unsqueeze(0).broadcast_to([P, N_EXP, F])).then_inc(const2_in, 16)
            act.dma_start(b2_wide[:, :, :], t["b2"].unsqueeze(0).broadcast_to([P, N_EXP, D])).then_inc(const2_in, 16)
            act.wait_ge(w_transposed, 1)
            nc.scalar.activation(w_t[:, :, :].rearrange("p a b -> p (a b)"), ps_s[:, :], ACT.Copy).then_inc(w_ready, 1)
            nc.scalar.activation(gate_t[:, :], ps_pt[:, 0:N_EXP], ACT.Copy).then_inc(w_ready, 1)

            def step(t_, k, phase, looping):
                p, kp = t_ - 1, k - 1
                if live(kp, phase, looping):
                    act.wait_ge(att["shifted"], p + 1)
                    a = prob[:, kp % 2, :, :].rearrange("p h k -> p (h k)")
                    nc.scalar.activation(a, a, ACT.Exp, scale=1.0 / ROOT).then_inc(att["probs_ready"], 1)
                p, kp = t_ + 2, k + 2
                if live(kp, phase, looping):
                    act.wait_ge(att["proj_done"], p + 1)
                    if kp >= 4:
                        act.wait_ge(att["pv_done"], p - 3)
                    else:
                        act.wait_ge(zeroed, 3)
                    for par in range(2):
                        nc.scalar.activation(
                            vb[64 * par:64 * par + 64, kp % 4, :, :, par, 0:DH],
                            ps_in[64 * par:64 * par + 64, 256:512].rearrange("p (b h e d) -> p b h e d", b=2, e=2, d=DH)[:, :, :, par, :],
                            ACT.Copy).then_inc(att["v_ready"], 1)
                p, kp = t_ - 2, k - 2
                if live(kp, phase, looping):
                    act.wait_ge(att["ot_done"], p + 1)
                    if kp >= 2:
                        act.wait_ge(att["y_done"], p - 1)
                    nc.scalar.activation(ot_sb[:, kp % 2, :], ps_y[:, 0:D], ACT.Copy).then_inc(att["ot_ready"], 1)
                p, kp = t_ - 1, k - 1
                if live(kp, phase, looping):
                    act.wait_ge(att["pt_done"], p + 1)
                    if kp >= 2:
                        act.wait_ge(att["pv_done"], p - 1)
                    nc.scalar.activation(probt[:, kp % 2, :, :].rearrange("p h q -> p (h q)"), ps_pt[:, :], ACT.Copy).then_inc(att["pt_ready"], 1)
                p, kp = t_ + 3, k + 3
                if live(kp, phase, looping):
                    act.wait_ge(att["in_done"], p + 1)
                    if kp >= 2:
                        act.wait_ge(att["proj_done"], p - 1)
                    n = 2 - phase
                    nc.scalar.activation(xct[:, kp % 2, 0:n, :].rearrange("p a b -> p (a b)"), ps_in[:, 0:n * D], ACT.Copy).then_inc(att["in_ready"], 1)
                p, kp = t_ - 3, k - 3
                if phase == 1 and live(kp, phase, looping):
                    act.wait_ge(att["tok_done"], p + 1 - NT)
                    if kp >= NT + 2:
                        act.wait_ge(att["logits_done"], p - 1 - NT)
                    nc.scalar.activation(tok_t[:, kp % 2, :], ps_in[:, 0:P], ACT.Copy).then_inc(att["tok_ready"], 1)
                    act.wait_ge(att["y_ready"], p + 1)
                    nc.scalar.activation(x_all[:, p - NT, :], res[:, kp % 4, 1, :], ACT.Copy).then_inc(moe["tok_kept"], 1)

            run_attention(act, 0, step)
            for g in range(2 * N_EXP):
                act.wait_ge(moe["w_turned"], g + 1)
                nc.scalar.activation(w_hi[g // N_EXP][:, g % N_EXP, :], ps_s[:, (g % 2) * F:(g % 2 + 1) * F], ACT.Copy).then_inc(moe["w_hi_ready"], 1)
            run_attention(act, 1, step)

            act.wait_ge(moe["route_exp"], 1)
            nc.scalar.activation(r_exp[:, :], r_sum[:, :], ACT.Exp).then_inc(moe["route_exp"], 1)

            def expert_step(t_, k, looping):
                p, kp = t_ + 1, k + 1
                if looping or 0 <= kp < NM:
                    act.wait_ge(moe["xt_done"], p + 1)
                    if kp >= 2:
                        act.wait_ge(moe["h_done"], p - 1)
                    nc.scalar.activation(x_hi[:, kp % 2, :], ps_in[:, 0:P], ACT.Copy).then_inc(moe["xhi_ready"], 1)
                p, kp = t_ - 1, k - 1
                if looping or 0 <= kp < NM:
                    act.wait_ge(moe["ht_done"], p + 1)
                    if kp >= 2:
                        act.wait_ge(moe["yy_done"], p - 1)
                    nc.scalar.activation(h_hi[:, kp % 2, :], ps_pt[:, F * (kp % 2):F * (kp % 2 + 1)], ACT.Relu).then_inc(moe["hhi_ready"], 1)

            run_tiles(act, NM, 2, 3, expert_step)

        @block.gpsimd
        def _(pool):
            pool.memset(vb[:, :, :, :, :, :].rearrange("p s b h e d -> p (s b h e d)"), 0.0).then_inc(zeroed, 1)
            for par in range(2):
                pool.wait_ge(zeroed, par + 1)
                pool.memset(vb[64 * par:64 * par + 64, :, :, :, par, DH:DH + 1], 1.0).then_inc(zeroed, 1)
            pool.wait_ge(zeroed, 3)
            pool.wait_ge(prep, 2)
            pool.wait_ge(row_ready, 1)

            def step(t_, k, phase, looping):
                p, kp = t_, k
                if phase == 0 and live(kp, phase, looping):
                    pool.wait_ge(att["max_ready"], p + 1)
                    a = prob[:, kp % 2, :, :]
                    nc.gpsimd.tensor_tensor(a, a, neg_max[:, kp % 2, :].unsqueeze(2).broadcast_to([P, H, S]), ALU.add).then_inc(att["shifted"], 1)
                p, kp = t_ + 4, k + 4
                if live(kp, phase, looping):
                    if phase == 0:
                        mv, rs = mv_a[:, kp % 2, :], rs_a[:, kp % 2, :]
                        wait_apart(pool, pool_passed, att["x_mv"], p + 1)
                        nc.gpsimd.tensor_scalar(rs[:, 0:1], mv[:, 1:2], EPS, None, ALU.add).then_inc(att["x_var"], 1)
                        pool.wait_ge(att["x_var"], p + 1)
                        nc.gpsimd.tensor_tensor(rs[:, 1:2], rs[:, 0:1], neg_half[:, :], ALU.pow).then_inc(att["x_rstd"], 1)
                    else:
                        if kp % (4 if looping else 8) == 0:
                            for n in range(4) if looping else [(kp - NT) // 8]:
                                pool.wait_ge(src_in[n], 32)
                        pool.wait_ge(att["in_done"], p - 1)
                        nc.gpsimd.tensor_copy(xn[:, kp % 2, :], src_all[:, p - NT, :]).then_inc(att["xn_ready"], 1)
                p, kp = t_ - 1, k - 1
                if live(kp, phase, looping):
                    a = (x_all, src_all)[phase][:, p - phase * NT, :]
                    pool.wait_ge(att["xn_ready"], p + 1)
                    nc.gpsimd.tensor_tensor(a, a, row_add[:, phase, :], ALU.add).then_inc(att["residual_ready"], 1)
                p, kp = t_ - 2, k - 2
                if live(kp, phase, looping):
                    mv, rs = mv_b[:, kp % 2, :], rs_b[:, kp % 2, :]
                    wait_apart(pool, pool_passed, att["y_mv"], p + 1)
                    nc.gpsimd.tensor_scalar(rs[:, 0:1], mv[:, 1:2], EPS, None, ALU.add).then_inc(att["y_var"], 1)
                    pool.wait_ge(att["y_var"], p + 1)
                    nc.gpsimd.tensor_tensor(rs[:, 1:2], rs[:, 0:1], neg_half[:, :], ALU.pow).then_inc(att["y_rstd"], 1)
                    z, zn = res[:, kp % 4, 0, :], res[:, kp % 4, 1, :]
                    if phase == 0:
                        wait_apart(pool, pool_passed, att["y_rstd"], p + 1)
                        nc.gpsimd.tensor_scalar(zn, z, mv[:, 0:1], rs[:, 1:2], ALU.subtract, ALU.mult).then_inc(att["y_ready"], 1)
                    else:
                        if kp >= NT + 4:
                            pool.wait_ge(att["tok_done"], p - 3 - NT)
                        q = p - NT
                        wait_apart(pool, pool_passed, att["y_rstd"], p + 1)
                        nc.gpsimd.tensor_scalar(zn, z, mv[:, 0:1], rs[:, 1:2], ALU.subtract, ALU.mult).then_inc(att["y_norm"], 1)
                        pool.wait_ge(att["y_norm"], q + 1)
                        nc.gpsimd.tensor_tensor(z, zn, ln1[:, 0, :], ALU.mult).then_inc(att["y_gain"], 1)
                        pool.wait_ge(att["y_gain"], q + 1)
                        nc.gpsimd.tensor_tensor(zn, z, ln1[:, 1, :], ALU.add).then_inc(att["y_ready"], 1)

            run_attention(pool, 0, step)
            run_attention(pool, 1, step)

            pool.wait_ge(blanked, 16)

            def pack_step(t_, kp, looping):
                p = t_
                wait_apart(pool, pool_passed, moe["tok_copied"], p + 1)
                wait_apart(pool, pool_passed, moe["idx_copied"], p + 1)
                for c in range(TOP):
                    nc.gpsimd.indirect_dma_start(
                        out=packed, out_offset=bass.IndirectOffsetOnAxis(ap=idx_slot[:, kp % 4, c:c + 1], axis=0),
                        in_=tok_slot[:, kp % 4, :], in_offset=None).then_inc(packed_out[kp % 4], 16)

            for n in range(4):
                pack_step(n, n, False)
            with pool.Fori(1, NT // 4) as i:
                for u in range(4):
                    pack_step(i * 4 + u, 4 + u, True)

            def combine_step(t_, k, looping):
                p, kp = t_ + 2, k + 2
                if looping or 0 <= kp < NT:
                    wait_apart(pool, pool_passed, moe["idx_copied"], NT + p + 1)
                    if kp >= 4:
                        wait_apart(pool, pool_passed, moe["z_ready"], p - 3)
                    for c in range(TOP):
                        nc.gpsimd.indirect_dma_start(
                            out=got[:, kp % 4, c, :], out_offset=None, in_=expert_out,
                            in_offset=bass.IndirectOffsetOnAxis(ap=idx_slot[:, kp % 4, c:c + 1], axis=0)).then_inc(got_in[kp % 4], 16)
                p, kp = t_, k
                if looping or 0 <= kp < NT:
                    pool.wait_ge(x1_read[kp % 4], 8 * (p - kp % 4) + 32)
                    nc.gpsimd.tensor_tensor(x1_in[:, kp % 4, :], x1_in[:, kp % 4, :], ln2[:, 1, :], ALU.add).then_inc(moe["x1_added"], 1)
                    mv, rs = mv_b[:, kp % 2, :], rs_b[:, kp % 2, :]
                    wait_apart(pool, pool_passed, moe["x1_added"], p + 1)
                    wait_apart(pool, pool_passed, moe["z_mv"], p + 1)
                    nc.gpsimd.tensor_scalar(rs[:, 0:1], mv[:, 1:2], EPS, None, ALU.add).then_inc(moe["z_var"], 1)
                    pool.wait_ge(moe["z_var"], p + 1)
                    nc.gpsimd.tensor_tensor(rs[:, 1:2], rs[:, 0:1], neg_half[:, :], ALU.pow).then_inc(moe["z_rstd"], 1)

            for n in range(4):
                pool.wait_ge(y_out[n], 16 * NM // 4)
            run_tiles(pool, NT, 1, 3, combine_step)

        @block.vector
        def _(dve):
            nc.vector.memset(zero_tile[:, :], 0.0).then_inc(zero_ready, 1)
            dve.wait_ge(const_in, 16 * 16)
            nc.vector.memset(neg_half[:, :], -0.5).then_inc(prep, 1)
            nc.vector.memset(ones[:, :], 1.0).then_inc(zero_ready, 1)
            nc.vector.tensor_scalar(decay[:, :], dist[:, :], td[:, :], -ROOT, ALU.mult, ALU.mult).then_inc(prep, 1)
            nc.vector.tensor_copy(bias_v_wide[:, :, :], bias_v[:, :].unsqueeze(2).broadcast_to([P, 2, P])).then_inc(row_done, 1)
            dve.wait_ge(row_done, 2)
            nc.vector.tensor_tensor(row_add[:, :, :], ps_o[:, 0:2 * D].rearrange("p (a b) -> p a b", a=2), bias_o[:, :, :], ALU.add).then_inc(row_ready, 1)
            dve.wait_ge(prep, 2)
            dve.wait_ge(x_in0, 16)
            loaded = [0]

            def step(t_, k, phase, looping):
                p, kp = t_ - 4, k - 4
                if phase == 1 and live(kp, phase, looping):
                    q = p - NT
                    dve.wait_ge(att["logits_done"], q + 1)
                    nc.vector.tensor_tensor(logit[:, q, :], ps_qk[:, 256:256 + N_EXP], bias_g[:, :], ALU.add).then_inc(att["logits_read"], 1)
                p, kp = t_, k
                if live(kp, phase, looping):
                    a = prob[:, kp % 2, :, :]
                    sc = ps_s[:, :].rearrange("p (h k) -> p h k", h=H)
                    dve.wait_ge(att["scores_done"], p + 1)
                    if kp >= 2:
                        dve.wait_ge(att["pt_done"], p - 1)
                        dve.wait_ge(att["shifted"], p - 1)
                    if phase == 0:
                        nc.vector.tensor_tensor(a, sc, decay[:, :].unsqueeze(1).broadcast_to([P, H, S]), ALU.add).then_inc(att["scores_read"], 1)
                        dve.wait_ge(att["scores_read"], p + 1)
                        nc.vector.tensor_reduce(neg_max[:, kp % 2, :], a, AX.X, ALU.max, negate=True).then_inc(att["max_ready"], 1)
                    else:
                        nc.vector.tensor_reduce(neg_max[:, kp % 2, :], sc, AX.X, ALU.max, negate=True).then_inc(att["max_ready"], 1)
                        dve.wait_ge(att["max_ready"], p + 1)
                        nc.vector.tensor_tensor(a, sc, neg_max[:, kp % 2, :].unsqueeze(2).broadcast_to([P, H, S]), ALU.add).then_inc(att["shifted"], 1)
                p, kp = t_ + 2, k + 2
                if live(kp, phase, looping):
                    dve.wait_ge(att["proj_done"], p + 1)
                    if kp >= 2:
                        dve.wait_ge(att["scores_done"], p - 1)
                    for n, (dst, mask) in enumerate(((qm, mask_q), (kx, mask_k))):
                        nc.vector.scalar_tensor_tensor(
                            out=dst[:, kp % 2, :, :], in0=ps_qk[:, n * P:n * P + P].unsqueeze(1).broadcast_to([P, G4, P]),
                            scalar=bias_qk[:, phase, n:n + 1], in1=mask[:, :].unsqueeze(2).broadcast_to([P, G4, P]),
                            op0=ALU.add, op1=ALU.mult).then_inc(att["qk_ready"], 1)
                p, kp = t_ + 4, k + 4
                if phase == 0 and live(kp, phase, looping):
                    if kp >= 8 and not loaded[0]:
                        dve.wait_ge(x_in1, 16)
                        loaded[0] = 1
                    if kp >= 2:
                        dve.wait_ge(att["xn_ready"], p - 1)
                    nc.vector.bn_stats(stats_a[:, kp % 2, :], x_all[:, p, :]).then_inc(att["x_stats"], 1)
                    wait_apart(dve, dve_passed, att["x_stats"], p + 1)
                    nc.vector.bn_aggr(mv_a[:, kp % 2, :], stats_a[:, kp % 2, :]).then_inc(att["x_mv"], 1)
                p, kp = t_ - 2, k - 2
                if live(kp, phase, looping):
                    dve.wait_ge(att["y_done"], p + 1)
                    dve.wait_ge(att["residual_ready"], p + 1)
                    if phase == 0:
                        if kp >= 4:
                            dve.wait_ge(stored[kp % 4], 4 * (p - kp % 4))
                    else:
                        dve.wait_ge(att["y_ready"], p - 3)
                        dve.wait_ge(stored[kp % 4], 16 * NT // 4)
                    z = res[:, kp % 4, 0, :]
                    nc.vector.tensor_tensor(z, ps_y[:, P:2 * P], (x_all, src_all)[phase][:, p - phase * NT, :], ALU.add).then_inc(att["y_read"], 1)
                    dve.wait_ge(att["y_read"], p + 1)
                    if kp >= 2:
                        dve.wait_ge(att["y_ready"], p - 1)
                    nc.vector.bn_stats(stats_b[:, kp % 2, :], z).then_inc(att["y_stats"], 1)
                    wait_apart(dve, dve_passed, att["y_stats"], p + 1)
                    nc.vector.bn_aggr(mv_b[:, kp % 2, :], stats_b[:, kp % 2, :]).then_inc(att["y_mv"], 1)
                p, kp = t_ - 1, k - 1
                if live(kp, phase, looping):
                    dve.wait_ge(att["pv_done"], p + 1)
                    o = ps_o[:, 0:H * (DH + 1)].rearrange("p (h c) -> p h c", h=H)
                    nc.vector.reciprocal(inv_sum[:, kp % 2, :].unsqueeze(2), o[:, :, DH:DH + 1]).then_inc(att["inv_ready"], 1)
                    dve.wait_ge(att["inv_ready"], p + 1)
                    if kp >= 2:
                        dve.wait_ge(att["ot_done"], p - 1)
                    nc.vector.tensor_tensor(o_sb[:, kp % 2, :].rearrange("p (h d) -> p h d", h=H), o[:, :, 0:DH],
                                            inv_sum[:, kp % 2, :].unsqueeze(2).broadcast_to([P, H, DH]), ALU.mult).then_inc(att["o_ready"], 1)
                p, kp = t_ + 4, k + 4
                if phase == 0 and live(kp, phase, looping):
                    dve.wait_ge(att["x_rstd"], p + 1)
                    if kp >= 2:
                        dve.wait_ge(att["in_done"], p - 1)
                    nc.vector.tensor_scalar(xn[:, kp % 2, :], x_all[:, p, :], mv_a[:, kp % 2, 0:1], rs_a[:, kp % 2, 1:2],
                                            ALU.subtract, ALU.mult).then_inc(att["xn_ready"], 1)

            run_attention(dve, 0, step)
            for g in range(2 * N_EXP):
                dve.wait_ge(moe["w_hi_ready"], g + 1)
                half = g // N_EXP
                nc.vector.tensor_tensor(w_lo[half][:, g % N_EXP, :], ps_s[:, (g % 2) * F:(g % 2 + 1) * F],
                                        w_hi[half][:, g % N_EXP, :].bitcast(FP32), ALU.subtract).then_inc(moe["w_lo_ready"], 1)
            run_attention(dve, 1, step)

            made = [0]

            def then(instruction):
                made[0] += 1
                instruction.then_inc(moe["route"], 1)
                dve.wait_ge(moe["route"], made[0])

            dve.wait_ge(const2_in, 16 * 8)
            dve.wait_ge(att["logits_read"], NT)
            v = nc.vector
            by_expert = rank8[:, :].unsqueeze(1).broadcast_to([P, NT, N_EXP])
            for c in range(TOP):
                left = rest if c else logit
                then(v.tensor_reduce(best[:, c, :], left[:, :, :], AX.X, ALU.max))
                then(v.tensor_tensor(r_key[:, :, :], left[:, :, :], best[:, c, :].unsqueeze(2).broadcast_to([P, NT, N_EXP]), ALU.is_equal))
                then(v.tensor_tensor(r_key[:, :, :], r_key[:, :, :], by_expert, ALU.mult))
                then(v.tensor_reduce(r_top[:, :], r_key[:, :, :], AX.X, ALU.max))
                then(v.tensor_tensor(pick[:, c, :, :], by_expert, r_top[:, :].unsqueeze(2).broadcast_to([P, NT, N_EXP]), ALU.is_equal))
                if c == 0:
                    flat = "p t e -> p (t e)"
                    then(v.scalar_tensor_tensor(out=rest[:, :, :].rearrange(flat), in0=pick[:, 0, :, :].rearrange(flat), scalar=-FAR,
                                                in1=logit[:, :, :].rearrange(flat), op0=ALU.mult, op1=ALU.add))
            then(v.tensor_tensor(both[:, :, :], pick[:, 0, :, :], pick[:, 1, :, :], ALU.add))
            v.tensor_tensor(r_sum[:, :], best[:, 1, :], best[:, 0, :], ALU.subtract).then_inc(moe["route_exp"], 1)
            dve.wait_ge(moe["counted"], 1)
            then(v.tensor_copy(scan[:, 0, :, :].rearrange(flat), ps_y[:, 0:NT * N_EXP]))
            side, gap = 0, 1
            while gap < NT:
                then(v.tensor_copy(scan[:, 1 - side, 0:gap, :], scan[:, side, 0:gap, :]))
                then(v.tensor_tensor(scan[:, 1 - side, gap:, :], scan[:, side, gap:, :], scan[:, side, 0:NT - gap, :], ALU.add))
                side, gap = 1 - side, 2 * gap
            total = scan[:, side, NT - 1, :]
            then(v.tensor_tensor(full[:, :, :], total.unsqueeze(2).broadcast_to([P, N_EXP, NT]),
                                 steps128[:, :].unsqueeze(1).broadcast_to([P, N_EXP, NT]), ALU.is_gt))
            then(v.tensor_reduce(tiles_of[:, :], full[:, :, :], AX.X, ALU.add))
            then(v.tensor_copy(tiles_to[:, 0, :], tiles_of[:, :]))
            at, gap = 0, 1
            while gap < N_EXP:
                then(v.tensor_copy(tiles_to[:, 1 - at, 0:gap], tiles_to[:, at, 0:gap]))
                then(v.tensor_tensor(tiles_to[:, 1 - at, gap:], tiles_to[:, at, gap:], tiles_to[:, at, 0:N_EXP - gap], ALU.add))
                at, gap = 1 - at, 2 * gap
            then(v.tensor_tensor(starts[:, :], tiles_to[:, at, :], tiles_of[:, :], ALU.subtract))
            then(v.tensor_scalar(starts[:, :], starts[:, :], float(P), None, ALU.mult))
            then(v.tensor_tensor(past[:, :, :], tile_no[:, :].unsqueeze(2).broadcast_to([P, NM, N_EXP]),
                                 tiles_to[:, at, :].unsqueeze(1).broadcast_to([P, NM, N_EXP]), ALU.is_ge))
            then(v.tensor_reduce(expert_f[:, :], past[:, :, 0:N_EXP - 1], AX.X, ALU.add))
            then(v.tensor_copy(expert_of[:, :], expert_f[:, :]))
            then(v.tensor_tensor(place[:, :, :].rearrange(flat), scan[:, side, :, :].rearrange(flat), ps_y[:, 0:NT * N_EXP], ALU.subtract))
            then(v.tensor_tensor(place[:, :, :].rearrange(flat), place[:, :, :].rearrange(flat), ps_o[:, 0:NT * N_EXP], ALU.add))
            then(v.tensor_tensor(place[:, :, :], place[:, :, :], starts[:, :].unsqueeze(1).broadcast_to([P, NT, N_EXP]), ALU.add))
            for c in range(TOP):
                then(v.tensor_tensor(r_key[:, :, :], place[:, :, :], pick[:, c, :, :], ALU.mult))
                then(v.tensor_reduce(slot_f[:, c, :], r_key[:, :, :], AX.X, ALU.add))
            then(v.tensor_copy(slot_u[:, :, :], slot_f[:, :, :]))
            dve.wait_ge(moe["route_exp"], 2)
            then(v.tensor_scalar(r_sum[:, :], r_exp[:, :], 1.0, None, ALU.add))
            then(v.reciprocal(share[:, 0, :], r_sum[:, :]))
            then(v.tensor_tensor(share[:, 1, :], share[:, 0, :], r_exp[:, :], ALU.mult))
            dve.wait_ge(moe["tok_kept"], NT)

            def pack_step(t_, kp, looping):
                p = t_
                if kp >= 4:
                    dve.wait_ge(packed_out[kp % 4], 8 * (p - kp % 4))
                v.tensor_copy(tok_slot[:, kp % 4, :], x_all[:, p, :]).then_inc(moe["tok_copied"], 1)
                v.tensor_copy(idx_slot[:, kp % 4, :].unsqueeze(2), slot_u[:, :, bass.ds(p, 1)]).then_inc(moe["idx_copied"], 1)

            for n in range(4):
                pack_step(n, n, False)
            with dve.Fori(1, NT // 4) as i:
                for u in range(4):
                    pack_step(i * 4 + u, 4 + u, True)

            def expert_step(t_, k, looping):
                p, kp = t_, k
                if looping or 0 <= kp < NM:
                    e = dve.value_load(expert_of[0:1, bass.ds(p, 1)], min_val=0, max_val=N_EXP - 1)
                    dve.wait_ge(moe["h_done"], p + 1)
                    if kp >= 2:
                        dve.wait_ge(moe["ht_done"], p - 1)
                    v.tensor_tensor(h_sb[:, kp % 2, :], ps_s[:, F * (kp % 2):F * (kp % 2 + 1)], b1_wide[:, e, :], ALU.add).then_inc(moe["hb_ready"], 1)
                p, kp = t_ + 1, k + 1
                if looping or 0 <= kp < NM:
                    dve.wait_ge(moe["xhi_ready"], p + 1)
                    v.tensor_tensor(x_lo[:, kp % 2, :], ps_in[:, 0:P], x_hi[:, kp % 2, :].bitcast(FP32), ALU.subtract).then_inc(moe["xlo_ready"], 1)
                p, kp = t_ - 1, k - 1
                if looping or 0 <= kp < NM:
                    dve.wait_ge(moe["hhi_ready"], p + 1)
                    v.scalar_tensor_tensor(out=h_lo[:, kp % 2, :], in0=ps_pt[:, F * (kp % 2):F * (kp % 2 + 1)], scalar=0.0,
                                           in1=h_hi[:, kp % 2, :].bitcast(FP32), op0=ALU.max, op1=ALU.subtract).then_inc(moe["hlo_ready"], 1)
                p, kp = t_ - 2, k - 2
                if looping or 0 <= kp < NM:
                    e = dve.value_load(expert_of[0:1, bass.ds(p, 1)], min_val=0, max_val=N_EXP - 1)
                    dve.wait_ge(moe["yy_done"], p + 1)
                    if kp >= 4:
                        dve.wait_ge(y_out[kp % 4], 4 * (p - kp % 4))
                    v.tensor_tensor(y_sb[:, kp % 4, :], (ps_o, ps_y)[kp % 2][:, 0:D], b2_wide[:, e, :], ALU.add).then_inc(moe["yo_ready"], 1)

            run_tiles(dve, NM, 2, 3, expert_step)

            def combine_step(t_, k, looping):
                p, kp = t_ + 3, k + 3
                if looping or 0 <= kp < NT:
                    if kp >= 4:
                        dve.wait_ge(got_in[kp % 4], 8 * (p - kp % 4))
                    v.tensor_copy(idx_slot[:, kp % 4, :].unsqueeze(2), slot_u[:, :, bass.ds(p, 1)]).then_inc(moe["idx_copied"], 1)
                p, kp = t_, k
                if looping or 0 <= kp < NT:
                    dve.wait_ge(got_in[kp % 4], 8 * (p - kp % 4) + 32)
                    z = z_sb[:, kp % 4, :]
                    v.scalar_tensor_tensor(out=z, in0=got[:, kp % 4, 0, :], scalar=share[:, 0, bass.ds(p, 1)], in1=x_all[:, p, :],
                                           op0=ALU.mult, op1=ALU.add).then_inc(moe["z_part"], 1)
                    dve.wait_ge(moe["z_part"], p + 1)
                    v.scalar_tensor_tensor(out=z, in0=got[:, kp % 4, 1, :], scalar=share[:, 1, bass.ds(p, 1)], in1=z,
                                           op0=ALU.mult, op1=ALU.add).then_inc(moe["z_ready"], 1)
                    dve.wait_ge(moe["z_ready"], p + 1)
                    v.bn_stats(stats_b[:, kp % 2, :], z).then_inc(moe["z_stats"], 1)
                    wait_apart(dve, dve_passed, moe["z_stats"], p + 1)
                    v.bn_aggr(mv_b[:, kp % 2, :], stats_b[:, kp % 2, :]).then_inc(moe["z_mv"], 1)
                p, kp = t_ - 1, k - 1
                if looping or 0 <= kp < NT:
                    z = z_sb[:, kp % 4, :]
                    dve.wait_ge(moe["z_rstd"], p + 1)
                    v.tensor_scalar(z, z, mv_b[:, kp % 2, 0:1], rs_b[:, kp % 2, 1:2], ALU.subtract, ALU.mult).then_inc(moe["z_norm"], 1)
                    dve.wait_ge(moe["z_norm"], p + 1)
                    v.tensor_tensor(z, z, ln2[:, 0, :], ALU.mult).then_inc(moe["z_gain"], 1)
                    dve.wait_ge(moe["z_gain"], p + 1)
                    dve.wait_ge(moe["x1_added"], p + 1)
                    if kp >= 4:
                        dve.wait_ge(out_done[kp % 4], 8 * (p - kp % 4))
                    v.tensor_tensor(o_out[:, kp % 4, :], z, x1_in[:, kp % 4, :], ALU.add).then_inc(moe["o_done"], 1)

            run_tiles(dve, NT, 1, 3, combine_step)

        @block.tensor
        def _(pe):
            pe.wait_ge(const_in, 16 * 16)
            pe.wait_ge(weights_in, 16 * 7)
            for n in range(8):
                nc.tensor.transpose(ps_s[:, n * D:(n + 1) * D], w_rows[:, n, :], ident[:, :])
            nc.tensor.transpose(ps_pt[:, 0:N_EXP], gate_rows[:, :], ident[0:N_EXP, 0:N_EXP]).then_inc(w_transposed, 1)
            pe.wait_ge(w_ready, 2)
            pe.wait_ge(row_done, 1)
            for n in range(2):
                m = nc.tensor.matmul(ps_o[:, n * D:(n + 1) * D], bias_v_wide[:, n, :], w_t[:, 4 * n + 3, :], start=True, stop=True)
            m.then_inc(row_done, 1)

            def step(t_, k, phase, looping):
                p, kp = t_ - 4, k - 4
                if phase == 1 and live(kp, phase, looping):
                    pe.wait_ge(att["tok_ready"], p + 1 - NT)
                    pe.wait_ge(att["qk_ready"], 2 * (p + 6) if looping or kp + 5 < 2 * NT else 4 * NT)
                    if kp >= NT + 1:
                        pe.wait_ge(att["logits_read"], p - NT)
                    nc.tensor.matmul(ps_qk[:, 256:256 + N_EXP], tok_t[:, kp % 2, :], gate_t[:, :], start=True, stop=True).then_inc(att["logits_done"], 1)
                p, kp = t_, k
                if live(kp, phase, looping):
                    pe.wait_ge(att["qk_ready"], 2 * p + 2)
                    if kp >= 1:
                        pe.wait_ge(att["shifted"] if phase else att["scores_read"], p)
                    for g in range(G4):
                        for b in range(2):
                            q = slice(64 * b, 64 * b + 64)
                            m = nc.tensor.matmul(ps_s[q, 256 * g:256 * g + 256], qm[:, kp % 2, g, q], kx[:, kp % 2, :, q], start=True, stop=True)
                    m.then_inc(att["scores_done"], 1)
                p, kp = t_ + 2, k + 2
                if live(kp, phase, looping):
                    pe.wait_ge(att["in_ready"], p + 1)
                    if kp >= 1:
                        pe.wait_ge(att["qk_ready"], 2 * p)
                        pe.wait_ge(att["v_ready"], 2 * p)
                    if phase == 1 and (looping or k - 4 >= NT):
                        pe.wait_ge(att["logits_read"], t_ - 3 - NT)
                        pe.wait_ge(att["tok_ready"], t_ - 3 - NT)
                    xt, ct = xct[:, kp % 2, 0, :], xct[:, kp % 2, 1 - phase, :]
                    w = 4 * phase
                    nc.tensor.matmul(ps_qk[:, 0:P], w_t[:, w, :], xt, start=True, stop=True)
                    nc.tensor.matmul(ps_qk[:, P:2 * P], w_t[:, w + 1, :], ct, start=True, stop=True)
                    for b in range(2):
                        for par in range(2):
                            m = nc.tensor.matmul(ps_in[64 * par:64 * par + 64, 256 + P * b:256 + P * b + P], ct[:, 64 * b:64 * b + 64], w_t[:, w + 2, :], start=True, stop=True)
                    m.then_inc(att["proj_done"], 1)
                p, kp = t_ - 2, k - 2
                if live(kp, phase, looping):
                    pe.wait_ge(att["o_ready"], p + 1)
                    if kp >= 1:
                        pe.wait_ge(att["y_read"], p)
                    nc.tensor.transpose(ps_y[:, 0:P], o_sb[:, kp % 2, :], ident[:, :]).then_inc(att["ot_done"], 1)
                p, kp = t_ - 1, k - 1
                if live(kp, phase, looping):
                    pe.wait_ge(att["probs_ready"], p + 1)
                    if kp >= 1:
                        pe.wait_ge(att["pt_ready"], p)
                    for h in range(H // 2):
                        m = nc.tensor.transpose(ps_pt[:, h * P:(h + 1) * P], prob[:, kp % 2, 2 * h:2 * h + 2, :], ident[:, :])
                    m.then_inc(att["pt_done"], 1)
                p, kp = t_ + 3, k + 3
                if live(kp, phase, looping):
                    pe.wait_ge(att["xn_ready"], p + 1)
                    if kp >= 1:
                        pe.wait_ge(att["v_ready"], 2 * p)
                        pe.wait_ge(att["in_ready"], p)
                    if phase == 1 and (looping or k - 4 >= NT):
                        pe.wait_ge(att["tok_ready"], t_ - 3 - NT)
                    if phase == 0:
                        pe.wait_ge(ctx_ready[kp % 4], 4 * (p - kp % 4) + 16)
                        nc.tensor.transpose(ps_in[:, P:2 * P], ctx_in[:, kp % 4, :], ident[:, :])
                    nc.tensor.transpose(ps_in[:, 0:P], xn[:, kp % 2, :], ident[:, :]).then_inc(att["in_done"], 1)
                p, kp = t_ - 2, k - 2
                if live(kp, phase, looping):
                    pe.wait_ge(att["ot_ready"], p + 1)
                    nc.tensor.matmul(ps_y[:, P:2 * P], ot_sb[:, kp % 2, :], w_t[:, 4 * phase + 3, :], start=True, stop=True).then_inc(att["y_done"], 1)
                p, kp = t_ - 1, k - 1
                if live(kp, phase, looping):
                    pe.wait_ge(att["pt_ready"], p + 1)
                    pe.wait_ge(att["v_ready"], 2 * p + 2)
                    if kp >= 1:
                        pe.wait_ge(att["o_ready"], p)
                    for h in range(H // 2):
                        for b in range(2):
                            m = nc.tensor.matmul(ps_o[64 * b:64 * b + 64, h * VW:(h + 1) * VW], probt[:, kp % 2, h, 64 * b:64 * b + 64],
                                                 vb[:, kp % 4, b, h, :, :], start=True, stop=True)
                    m.then_inc(att["pv_done"], 1)
                p, kp = t_ - 3, k - 3
                if phase == 1 and live(kp, phase, looping):
                    pe.wait_ge(att["y_ready"], p + 1)
                    pe.wait_ge(att["in_ready"], t_ + 4 if looping or k + 3 < 2 * NT else 2 * NT)
                    pe.wait_ge(att["v_ready"], 2 * t_ + 6 if looping or k + 2 < 2 * NT else 4 * NT)
                    nc.tensor.transpose(ps_in[:, 0:P], res[:, kp % 4, 1, :], ident[:, :]).then_inc(att["tok_done"], 1)

            run_attention(pe, 0, step)
            pe.wait_ge(expert_rows_in, 32)
            pe.wait_ge(att["scores_read"], NT)
            for g in range(2 * N_EXP):
                if g >= 2:
                    pe.wait_ge(moe["w_lo_ready"], g - 1)
                e = g % N_EXP
                for c in range(FC):
                    rows = w2_rows[:, e, c * P:(c + 1) * P] if g >= N_EXP else w1_rows[:, e * FC + c, :]
                    m = nc.tensor.transpose(ps_s[:, (g % 2) * F + c * P:(g % 2) * F + (c + 1) * P], rows, ident[:, :])
                m.then_inc(moe["w_turned"], 1)
            pe.wait_ge(moe["w_lo_ready"], 2 * N_EXP)
            run_attention(pe, 1, step)

            pe.wait_ge(const2_in, 16 * 8)
            pe.wait_ge(zero_ready, 2)
            pe.wait_ge(moe["route"], 12)
            picked = both[:, :, :].rearrange("p t e -> p (t e)")
            nc.tensor.matmul(ps_o[:, 0:NT * N_EXP], earlier[:, :], picked, start=True, stop=True)
            nc.tensor.matmul(ps_y[:, 0:NT * N_EXP], ones[:, :], picked, start=True, stop=True).then_inc(moe["counted"], 1)
            pe.wait_ge(moe["idx_copied"], 1)

            def expert_step(t_, k, looping):
                p, kp = t_, k
                if looping or 0 <= kp < NM:
                    e = pe.value_load(expert_of[0:1, bass.ds(p, 1)], min_val=0, max_val=N_EXP - 1)
                    pe.wait_ge(moe["xlo_ready"], p + 1)
                    if kp >= 2:
                        pe.wait_ge(moe["hb_ready"], p - 1)
                    a = ps_s[:, F * (kp % 2):F * (kp % 2 + 1)]
                    nc.tensor.matmul(a, x_lo[:, kp % 2, :], w_hi[0][:, e, :], start=True, stop=False)
                    nc.tensor.matmul(a, x_hi[:, kp % 2, :], w_lo[0][:, e, :], start=False, stop=False)
                    nc.tensor.matmul(a, x_hi[:, kp % 2, :], w_hi[0][:, e, :], start=False, stop=True).then_inc(moe["h_done"], 1)
                p, kp = t_ + 1, k + 1
                if looping or 0 <= kp < NM:
                    pe.wait_ge(xs_in[kp % 4], 4 * (p - kp % 4) + 16)
                    if kp >= 1:
                        pe.wait_ge(moe["xlo_ready"], p)
                    nc.tensor.transpose(ps_in[:, 0:P], xs[:, kp % 4, :], ident[:, :]).then_inc(moe["xt_done"], 1)
                p, kp = t_ - 1, k - 1
                if looping or 0 <= kp < NM:
                    pe.wait_ge(moe["hb_ready"], p + 1)
                    if kp >= 2:
                        pe.wait_ge(moe["hlo_ready"], p - 1)
                    for c in range(FC):
                        m = nc.tensor.transpose(ps_pt[:, F * (kp % 2) + c * P:F * (kp % 2) + (c + 1) * P], h_sb[:, kp % 2, c * P:(c + 1) * P], ident[:, :])
                    m.then_inc(moe["ht_done"], 1)
                p, kp = t_ - 2, k - 2
                if looping or 0 <= kp < NM:
                    e = pe.value_load(expert_of[0:1, bass.ds(p, 1)], min_val=0, max_val=N_EXP - 1)
                    pe.wait_ge(moe["hlo_ready"], p + 1)
                    if kp >= 2:
                        pe.wait_ge(moe["yo_ready"], p - 1)
                    a = (ps_o, ps_y)[kp % 2][:, 0:D]
                    n = 0
                    for h, w in ((h_lo, w_hi[1]), (h_hi, w_lo[1]), (h_hi, w_hi[1])):
                        for c in range(FC):
                            m = nc.tensor.matmul(a, h[:, kp % 2, c * P:(c + 1) * P], w[:, e, c * P:(c + 1) * P], start=n == 0, stop=n == 3 * FC - 1)
                            n += 1
                    m.then_inc(moe["yy_done"], 1)

            run_tiles(pe, NM, 2, 3, expert_step)


_SHORT = {"x": "x", "ctx_1024": "ctx"}


def kernel(**inputs):
    import numpy as _np
    import concourse.bacc as _bacc
    from concourse import mybir as _mybir
    from concourse.bass_utils import run_bass_kernel_spmd as _run

    nc = _bacc.Bacc("TRN2", target_bir_lowering=False, num_devices=1)
    arrays, t = {}, {}
    part = _np.arange(P)
    constants = {
        "ident": _np.eye(P, dtype=_np.float32),
        "dist": _np.abs(part[:, None] % S - _np.arange(S)[None, :]).astype(_np.float32),
        "mask_q": (part[:, None] // 32 == _np.arange(G4)[None, :]).astype(_np.float32),
        "earlier": (part[:, None] < part[None, :]).astype(_np.float32),
        "rank8": _np.tile(N_EXP - _np.arange(N_EXP, dtype=_np.float32), (P, 1)),
        "steps128": _np.tile(_np.arange(NT, dtype=_np.float32) * P, (P, 1)),
        "tile_no": _np.tile(_np.arange(NM, dtype=_np.float32), (P, 1)),
        "mask_k": (part[:, None] // DH % G4 == _np.arange(G4)[None, :]).astype(_np.float32),
    }
    for name, a in {**inputs, **constants}.items():
        a = _np.ascontiguousarray(a)
        if a.ndim == 0:
            a = a.reshape(1, 1)
        short = _SHORT.get(name, name.replace("L0_xattn_", "").replace("L0_ffn_", ""))
        arrays[f"in_{short}"] = a
        t[short] = nc.dram_tensor(f"in_{short}", a.shape, _mybir.dt.from_np(a.dtype), kind="ExternalInput").ap()
    out = nc.dram_tensor("out_0", (B, S, D), FP32, kind="ExternalOutput").ap()
    scratch = nc.dram_tensor("scratch", (B * S, 2, D), FP32).ap()
    packed = nc.dram_tensor("packed", (NM * P, D), FP32).ap()
    expert_out = nc.dram_tensor("expert_out", (NM * P, D), FP32).ap()
    build(nc, t, out, scratch, packed, expert_out)
    r = _run(nc, [arrays], core_ids=[0])
    return r.results[0]["out_0"]
```

```python
import concourse.bass as bass
from concourse import mybir
from contextlib import ExitStack

FP32 = mybir.dt.float32
FP32R = mybir.dt.float32r
UINT32 = mybir.dt.uint32
INT32 = mybir.dt.int32
ALU = mybir.AluOpType
ACT = mybir.ActivationFunctionType
AX = mybir.AxisListType

B, S, D = 64, 64, 128
H = 16
DH = D // H
P = 128
NT = B * S // P
G4 = 4
VW = 2 * (DH + 1)
EPS = 1e-5
ROOT = float(DH) ** 0.5
N_EXP, F = 8, 512
FC = F // P
TOP = 2
W_PART = 2 * N_EXP * F // NT
NM = (TOP * B * S + N_EXP * (P - 1)) // P
NM += -NM % 4
FAR = 3.0e38
WIDTHS = (P, S, G4, G4, P, N_EXP, NT, NM)
SHAPES = [(sum(WIDTHS[:n]), sum(WIDTHS[:n + 1])) for n in range(len(WIDTHS))]
SHAPES_END = sum(WIDTHS)


def build(nc, t, out, scratch, packed, expert_out):
    ctx = ExitStack()
    with ctx:
        def sb(name, shape, dt=FP32):
            return ctx.enter_context(nc.sbuf_tensor(name, shape, dt))

        def ps(name, cols):
            return ctx.enter_context(nc.psum_tensor(name, [P, cols], FP32))

        def sem(name):
            return ctx.enter_context(nc.semaphore(name))

        shapes = sb("shapes", [P, SHAPES_END])
        ident, dist, mask_q, mask_k, earlier, rank8, steps128, tile_no = (
            shapes[:, a:b] for a, b in SHAPES)
        neg_half = sb("neg_half", [P, 1])
        decay = sb("decay", [P, S])
        td = sb("td", [P, 1])
        w_t = sb("w_t", [P, 8, D])
        gate_t = sb("gate_t", [P, N_EXP])
        columns = sb("columns", [P, 6])
        bias_qk = columns[:, 0:4].rearrange("p (a b) -> p a b", a=2)
        bias_v = columns[:, 4:6]
        rows = sb("rows", [P, 6, D])
        bias_o, ln1, ln2 = rows[:, 0:2, :], rows[:, 2:4, :], rows[:, 4:6, :]
        bias_v_wide = sb("bias_v_wide", [P, 2, P])
        bias_g = sb("bias_g", [P, N_EXP])
        row_add = sb("row_add", [P, 2, D])
        w_hi = sb("w_hi", [P, 2, N_EXP, F], FP32R)
        w_lo = sb("w_lo", [P, 2, N_EXP, F], FP32R)
        b1_wide = sb("b1_wide", [P, N_EXP, F])
        b2_wide = sb("b2_wide", [P, N_EXP, D])
        zero_tile = sb("zero_tile", [P, D])
        ones = sb("ones", [P, P])
        x_all = sb("x_all", [P, NT, D])
        src_all = sb("src_all", [P, NT, D])
        ctx_in = sb("ctx_in", [P, 4, D])
        xn = sb("xn", [P, 2, D])
        xct = sb("xct", [P, 2, 2, D])
        qm = sb("qm", [P, 2, G4, P])
        kx = sb("kx", [P, 2, G4, P])
        vb = sb("vb", [P, 4, 2, H // 2, 2, DH + 1])
        prob = sb("prob", [P, 2, H, S])
        probt = sb("probt", [P, 2, H // 2, P])
        neg_max = sb("neg_max", [P, 2, H])
        inv_sum = sb("inv_sum", [P, 2, H])
        o_sb = sb("o_sb", [P, 2, D])
        ot_sb = sb("ot_sb", [P, 2, D])
        stats_a = sb("stats_a", [P, 2, 6])
        mv_a = sb("mv_a", [P, 2, 2])
        rs_a = sb("rs_a", [P, 2, 2])
        stats_b = sb("stats_b", [P, 2, 6])
        mv_b = sb("mv_b", [P, 2, 2])
        rs_b = sb("rs_b", [P, 2, 2])
        res = sb("res", [P, 4, 2, D])
        tok_t = sb("tok_t", [P, 2, P])
        logit = sb("logit", [P, NT, N_EXP])
        with ExitStack() as early:
            w_given = early.enter_context(nc.sbuf_tensor("w_given", [P, 2 * N_EXP * F], FP32))
        best = sb("best", [P, TOP, NT])
        pick = sb("pick", [P, TOP, NT, N_EXP])
        r_key = sb("r_key", [P, NT, N_EXP])
        r_top = sb("r_top", [P, NT])
        rest = sb("rest", [P, NT, N_EXP])
        both = sb("both", [P, NT, N_EXP])
        scan = sb("scan", [P, 2, NT, N_EXP])
        place = sb("place", [P, NT, N_EXP])
        slot_f = sb("slot_f", [P, TOP, NT])
        slot_u = sb("slot_u", [P, TOP, NT], UINT32)
        share = sb("share", [P, TOP, NT])
        r_exp = sb("r_exp", [P, NT])
        r_sum = sb("r_sum", [P, NT])
        full = sb("full", [P, N_EXP, NT])
        tiles_of = sb("tiles_of", [P, N_EXP])
        tiles_to = sb("tiles_to", [P, 2, N_EXP])
        starts = sb("starts", [P, N_EXP])
        past = sb("past", [P, NM, N_EXP])
        expert_f = sb("expert_f", [P, NM])
        expert_of = sb("expert_of", [P, NM], INT32)
        tok_slot = sb("tok_slot", [P, 4, D])
        idx_slot = sb("idx_slot", [P, 4, TOP], UINT32)
        xs = sb("xs", [P, 4, D])
        x_hi = sb("x_hi", [P, 2, P], FP32R)
        x_lo = sb("x_lo", [P, 2, P], FP32R)
        h_hi = sb("h_hi", [P, 2, F], FP32R)
        h_lo = sb("h_lo", [P, 2, F], FP32R)

        flat_a = prob[:, :, :, :].rearrange("p s h k -> p (s h k)")
        flat_b = probt[:, :, :, :].rearrange("p s h q -> p (s h q)")
        got = flat_a[:, 0:8 * D].rearrange("p (s c d) -> p s c d", s=4, c=TOP)
        x1_in = flat_a[:, 8 * D:12 * D].rearrange("p (s d) -> p s d", s=4)
        z_sb = flat_a[:, 12 * D:16 * D].rearrange("p (s d) -> p s d", s=4)
        h_sb = flat_b[:, 0:2 * F].rearrange("p (s f) -> p s f", s=2)
        y_sb = flat_b[:, 8 * D:12 * D].rearrange("p (s d) -> p s d", s=4)
        o_out = flat_b[:, 12 * D:16 * D].rearrange("p (s d) -> p s d", s=4)

        ps_in = ps("ps_in", 512)
        ps_qk = ps("ps_qk", 512)
        ps_s = ps("ps_s", 1024)
        ps_pt = ps("ps_pt", 1024)
        ps_o = ps("ps_o", 512)
        ps_y = ps("ps_y", 512)

        const2_in = sem("const2_in")
        weights_in, const_in, x_in0, x_in1 = sem("weights_in"), sem("const_in"), sem("x_in0"), sem("x_in1")
        src_in = [sem(f"src_in{n}") for n in range(4)]
        zeroed, row_done, prep = sem("zeroed"), sem("row_done"), sem("prep")
        row_ready = sem("row_ready")
        ctx_ready = [sem(f"ctx_ready{n}") for n in range(4)]
        stored = [sem(f"stored{n}") for n in range(4)]
        names = ("x_stats x_mv x_var x_rstd xn_ready residual_ready in_done in_ready proj_done qk_ready "
                 "v_ready scores_done scores_read max_ready shifted probs_ready pt_done pt_ready pv_done "
                 "inv_ready o_ready ot_done ot_ready y_done y_read y_stats y_mv y_var y_rstd y_norm y_gain "
                 "y_ready tok_done tok_ready logits_done logits_read").split()
        att = {n: sem(n) for n in names}
        names = ("w_hi_ready w_lo_ready counted route_exp route "
                 "xt_done xhi_ready xlo_ready h_done hb_ready ht_done hhi_ready hlo_ready yy_done yo_ready "
                 "tok_copied idx_copied z_part z_ready z_stats z_mv z_var z_rstd z_norm z_gain o_done x1_added tok_kept").split()
        moe = {n: sem(n) for n in names}
        blanked, zero_ready = sem("blanked"), sem("zero_ready")
        expert_w_in = [sem(f"expert_w_in{n}") for n in range(4)]
        packed_out = [sem(f"packed_out{n}") for n in range(4)]
        xs_in = [sem(f"xs_in{n}") for n in range(4)]
        y_out = [sem(f"y_out{n}") for n in range(4)]
        got_in = [sem(f"got_in{n}") for n in range(4)]
        x1_read = [sem(f"x1_read{n}") for n in range(4)]
        out_done = [sem(f"out_done{n}") for n in range(4)]
        dve_passed, pool_passed = sem("dve_passed"), sem("pool_passed")

        CONSTANTS = 6
        flat_w = "p n e f -> p (n e f)"

        block = ctx.enter_context(nc.Block())

        def run_attention(eng, phase, step):
            first = phase * NT
            for n in range(-4, 8):
                step(first + n, first + n, phase, False)
            with eng.Fori(2, NT // 4 - 1) as i:
                for u in range(4):
                    step(i * 4 + (first + u), first + 8 + u, phase, True)
            for n in range(NT - 4, NT + 6):
                step(first + n, first + n, phase, False)

        def run_tiles(eng, count, behind, ahead, step):
            for n in range(-ahead, 8):
                step(n, n, False)
            with eng.Fori(2, count // 4 - 1) as i:
                for u in range(4):
                    step(i * 4 + u, 8 + u, True)
            for n in range(count - 4, count + behind):
                step(n, n, False)

        def wait_apart(eng, passed, semaphore, value):
            eng.wait_ge(semaphore, value)
            eng.sem_inc(passed, 1)

        IN_RANGE = "the experts' numbers are counts of at most N_EXP - 1 terms that are 0 or 1"

        def load_experts(eng, t_, k, looping, regs):
            if looping and k % 4:
                return
            if looping or k in (0, NM - 4):
                first, count = (0, 8) if k == 0 else (t_ - 2, 6)
                _, values = nc.values_load_multi_w_load_instructions(
                    expert_of[0:1, bass.ds(first, count)], [eng], min_val=0, max_val=N_EXP - 1,
                    skip_runtime_bounds_check_because=IN_RANGE)
                regs.clear()
                regs.update((k + n - (0 if k == 0 else 2), value) for n, value in enumerate(values))

        def live(k, phase, looping):
            return looping or 0 <= k - phase * NT < NT

        @block.sync
        def _(sp):
            sp.dma_start(shapes[:, :], t["shapes"]).then_inc(const_in, 16)
            sp.dma_start(w_t[:, :, :], t["weights"]).then_inc(weights_in, 16)
            x_v = t["x"].rearrange("b s d -> (b s) d").rearrange("(n p) d -> p n d", p=P)
            c_v = t["ctx"].rearrange("b s d -> (b s) d")
            b1_v = t["b1"].rearrange("e f -> (e f)")
            packed_v = packed.rearrange("(n p) d -> p n d", p=P)

            def step(t_, k, phase, looping):
                p, kp = t_ + 4, k + 4
                if phase == 0 and live(kp, phase, looping):
                    if kp >= 4:
                        sp.wait_ge(att["in_done"], p - 3)
                    sp.dma_start(ctx_in[:, kp % 4, :], c_v[bass.ds(p * P, P), :]).then_inc(ctx_ready[kp % 4], 16)
                p, kp = t_ - 3, k - 3
                if phase == 0 and live(kp, phase, looping):
                    sp.wait_ge(att["y_ready"], p + 1)
                    sp.dma_start(scratch[bass.ds(p * P, P), :, :], res[:, kp % 4, :, :]).then_inc(stored[kp % 4], 16)
                p, kp = t_, k
                if phase == 0 and live(kp, phase, looping):
                    if kp == 0:
                        sp.dma_start(x_all[:, 8:NT, :], x_v[:, 8:NT, :]).then_inc(x_in1, 16)
                        sp.wait_ge(zero_ready, 1)
                    sp.dma_start(w_given[:, bass.ds(p * W_PART, W_PART)], t["expert_w"][:, bass.ds(p * W_PART, W_PART)]).then_inc(expert_w_in[kp % 4], 16)
                    sp.dma_start(b1_wide[:, :, :].rearrange("p e f -> p (e f)")[:, bass.ds(p * P, P)],
                                 b1_v[bass.ds(p * P, P)].unsqueeze(0).broadcast_to([P, P])).then_inc(const2_in, 16)
                    sp.dma_start(packed_v[:, bass.ds(p * 2, 2), :], zero_tile[:, :].unsqueeze(1).broadcast_to([P, 2, D])).then_inc(blanked, 16)

            run_attention(sp, 0, step)
            sp.dma_start(packed_v[:, 2 * NT:NM, :], zero_tile[:, :].unsqueeze(1).broadcast_to([P, NM - 2 * NT, D])).then_inc(blanked, 16)
            for n in range(4):
                sp.wait_ge(stored[n], 16 * NT // 4)
            s_v = scratch.rearrange("(i r c) a d -> c i r a d", i=B, c=2)
            for n in range(4):
                for c in range(2):
                    sp.dma_start(src_all[c * 64:c * 64 + 64, 8 * n:8 * n + 8, :], s_v[c, :, 8 * n:8 * n + 8, 1, :]).then_inc(src_in[n], 16)

            for n in range(4):
                sp.wait_ge(packed_out[n], 2 * 16 * NT // 4)

            def expert_step(t_, k, looping):
                p, kp = t_ + 3, k + 3
                if looping or 0 <= kp < NM:
                    if kp >= 4:
                        sp.wait_ge(moe["xt_done"], p - 3)
                    sp.dma_start(xs[:, kp % 4, :], packed[bass.ds(p * P, P), :]).then_inc(xs_in[kp % 4], 16)
                p, kp = t_ - 2, k - 2
                if looping or 0 <= kp < NM:
                    sp.wait_ge(moe["yo_ready"], p + 1)
                    sp.dma_start(expert_out[bass.ds(p * P, P), :], y_sb[:, kp % 4, :]).then_inc(y_out[kp % 4], 16)

            run_tiles(sp, NM, 2, 3, expert_step)

            x1_v = scratch.rearrange("(i r c) a d -> c r i a d", i=B, c=2)
            out_v = out.rearrange("i (r c) d -> c r i d", c=2)

            def combine_step(t_, k, looping):
                p, kp = t_ + 3, k + 3
                if looping or 0 <= kp < NT:
                    if kp >= 4:
                        sp.wait_ge(moe["o_done"], p - 3)
                    for c in range(2):
                        sp.dma_start(x1_in[64 * c:64 * c + 64, kp % 4, :], x1_v[c, p, :, 0, :]).then_inc(x1_read[kp % 4], 16)
                p, kp = t_ - 1, k - 1
                if looping or 0 <= kp < NT:
                    sp.wait_ge(moe["o_done"], p + 1)
                    for c in range(2):
                        sp.dma_start(out_v[c, p, :, :], o_out[64 * c:64 * c + 64, kp % 4, :]).then_inc(out_done[kp % 4], 16)

            run_tiles(sp, NT, 1, 3, combine_step)
            for n in range(4):
                sp.wait_ge(out_done[n], 2 * 16 * NT // 4)

        @block.scalar
        def _(act):
            act.dma_start(x_all[:, 0:8, :], t["x"].rearrange("b s d -> (b s) d").rearrange("(n p) d -> p n d", p=P)[:, 0:8, :]).then_inc(x_in0, 16)
            act.dma_start(columns[:, :], t["columns"]).then_inc(const_in, 16)
            act.dma_start(td[:, :], t["time_decay"].broadcast_to([P, 1])).then_inc(const_in, 16)
            act.dma_start(rows[:, :, :], t["rows"].unsqueeze(0).broadcast_to([P, 6, D])).then_inc(const_in, 16)
            act.dma_start(bias_g[:, :], t["gate_b"].unsqueeze(0).broadcast_to([P, N_EXP])).then_inc(const_in, 16)
            act.dma_start(gate_t[:, :], t["gate_w"]).then_inc(const_in, 16)
            act.dma_start(b2_wide[:, :, :], t["b2"].unsqueeze(0).broadcast_to([P, N_EXP, D])).then_inc(const2_in, 16)

            def step(t_, k, phase, looping):
                p, kp = t_ - 1, k - 1
                if live(kp, phase, looping):
                    act.wait_ge(att["shifted"], p + 1)
                    a = prob[:, kp % 2, :, :].rearrange("p h k -> p (h k)")
                    nc.scalar.activation(a, a, ACT.Exp, scale=1.0 / ROOT).then_inc(att["probs_ready"], 1)
                p, kp = t_ - 5, k - 5
                if phase == 1 and live(kp, phase, looping):
                    act.wait_ge(att["tok_done"], p + 1 - NT)
                    if kp >= NT + 2:
                        act.wait_ge(att["logits_done"], p - 1 - NT)
                    nc.scalar.activation(tok_t[:, kp % 2, :], ps_in[:, 0:P], ACT.Copy).then_inc(att["tok_ready"], 1)
                    act.wait_ge(att["y_ready"], p + 1)
                    nc.scalar.activation(x_all[:, p - NT, :], res[:, kp % 4, 1, :], ACT.Copy).then_inc(moe["tok_kept"], 1)
                p, kp = t_ + 2, k + 2
                if live(kp, phase, looping):
                    act.wait_ge(att["proj_done"], p + 1)
                    if kp >= 4:
                        act.wait_ge(att["pv_done"], p - 3)
                    else:
                        act.wait_ge(zeroed, 3)
                    for par in range(2):
                        nc.scalar.activation(
                            vb[64 * par:64 * par + 64, kp % 4, :, :, par, 0:DH],
                            ps_in[64 * par:64 * par + 64, 256:512].rearrange("p (b h e d) -> p b h e d", b=2, e=2, d=DH)[:, :, :, par, :],
                            ACT.Copy).then_inc(att["v_ready"], 1)
                p, kp = t_ - 3, k - 3
                if live(kp, phase, looping):
                    act.wait_ge(att["ot_done"], p + 1)
                    if kp >= 2:
                        act.wait_ge(att["y_done"], p - 1)
                    nc.scalar.activation(ot_sb[:, kp % 2, :], ps_y[:, 0:D], ACT.Copy).then_inc(att["ot_ready"], 1)
                p, kp = t_ - 1, k - 1
                if live(kp, phase, looping):
                    act.wait_ge(att["pt_done"], p + 1)
                    if kp >= 2:
                        act.wait_ge(att["pv_done"], p - 1)
                    nc.scalar.activation(probt[:, kp % 2, :, :].rearrange("p h q -> p (h q)"), ps_pt[:, :], ACT.Copy).then_inc(att["pt_ready"], 1)
                p, kp = t_ + 3, k + 3
                if live(kp, phase, looping):
                    act.wait_ge(att["in_done"], p + 1)
                    if kp >= 2:
                        act.wait_ge(att["proj_done"], p - 1)
                    n = 2 - phase
                    nc.scalar.activation(xct[:, kp % 2, 0:n, :].rearrange("p a b -> p (a b)"), ps_in[:, 0:n * D], ACT.Copy).then_inc(att["in_ready"], 1)
                p, kp = t_ - 2, k - 2
                if phase == 0 and live(kp, phase, looping):
                    act.wait_ge(expert_w_in[kp % 4], 4 * (p - kp % 4) + 16)
                    part = bass.ds(p * W_PART, W_PART)
                    nc.scalar.activation(w_hi[:, :, :, :].rearrange(flat_w)[:, part], w_given[:, part], ACT.Copy).then_inc(moe["w_hi_ready"], 1)

            run_attention(act, 0, step)
            run_attention(act, 1, step)

            act.wait_ge(moe["route_exp"], 1)
            nc.scalar.activation(r_exp[:, :], r_sum[:, :], ACT.Exp).then_inc(moe["route_exp"], 1)

            def expert_step(t_, k, looping):
                p, kp = t_ + 1, k + 1
                if looping or 0 <= kp < NM:
                    act.wait_ge(moe["xt_done"], p + 1)
                    if kp >= 2:
                        act.wait_ge(moe["h_done"], p - 1)
                    nc.scalar.activation(x_hi[:, kp % 2, :], ps_in[:, 0:P], ACT.Copy).then_inc(moe["xhi_ready"], 1)
                p, kp = t_ - 1, k - 1
                if looping or 0 <= kp < NM:
                    act.wait_ge(moe["ht_done"], p + 1)
                    if kp >= 2:
                        act.wait_ge(moe["yy_done"], p - 1)
                    nc.scalar.activation(h_hi[:, kp % 2, :], ps_pt[:, F * (kp % 2):F * (kp % 2 + 1)], ACT.Relu).then_inc(moe["hhi_ready"], 1)

            run_tiles(act, NM, 2, 3, expert_step)

        @block.gpsimd
        def _(pool):
            pool.memset(vb[:, :, :, :, :, :].rearrange("p s b h e d -> p (s b h e d)"), 0.0).then_inc(zeroed, 1)
            for par in range(2):
                pool.wait_ge(zeroed, par + 1)
                pool.memset(vb[64 * par:64 * par + 64, :, :, :, par, DH:DH + 1], 1.0).then_inc(zeroed, 1)
            pool.wait_ge(zeroed, 3)
            pool.wait_ge(prep, 2)
            pool.wait_ge(row_ready, 1)

            def step(t_, k, phase, looping):
                p, kp = t_, k
                if phase == 0 and live(kp, phase, looping):
                    pool.wait_ge(att["max_ready"], p + 1)
                    a = prob[:, kp % 2, :, :]
                    nc.gpsimd.tensor_tensor(a, a, neg_max[:, kp % 2, :].unsqueeze(2).broadcast_to([P, H, S]), ALU.add).then_inc(att["shifted"], 1)
                p, kp = t_ + 4, k + 4
                if live(kp, phase, looping):
                    if phase == 0:
                        mv, rs = mv_a[:, kp % 2, :], rs_a[:, kp % 2, :]
                        wait_apart(pool, pool_passed, att["x_mv"], p + 1)
                        nc.gpsimd.tensor_scalar(rs[:, 0:1], mv[:, 1:2], EPS, None, ALU.add).then_inc(att["x_var"], 1)
                        pool.wait_ge(att["x_var"], p + 1)
                        nc.gpsimd.tensor_tensor(rs[:, 1:2], rs[:, 0:1], neg_half[:, :], ALU.pow).then_inc(att["x_rstd"], 1)
                    else:
                        if kp % (4 if looping else 8) == 0:
                            for n in range(4) if looping else [(kp - NT) // 8]:
                                pool.wait_ge(src_in[n], 32)
                        pool.wait_ge(att["in_done"], p - 1)
                        nc.gpsimd.tensor_copy(xn[:, kp % 2, :], src_all[:, p - NT, :]).then_inc(att["xn_ready"], 1)
                p, kp = t_ - 2, k - 2
                if live(kp, phase, looping):
                    a = (x_all, src_all)[phase][:, p - phase * NT, :]
                    pool.wait_ge(att["xn_ready"], p + 1)
                    nc.gpsimd.tensor_tensor(a, a, row_add[:, phase, :], ALU.add).then_inc(att["residual_ready"], 1)
                p, kp = t_ - 3, k - 3
                if live(kp, phase, looping):
                    mv, rs = mv_b[:, kp % 2, :], rs_b[:, kp % 2, :]
                    wait_apart(pool, pool_passed, att["y_mv"], p + 1)
                    nc.gpsimd.tensor_scalar(rs[:, 0:1], mv[:, 1:2], EPS, None, ALU.add).then_inc(att["y_var"], 1)
                    pool.wait_ge(att["y_var"], p + 1)
                    nc.gpsimd.tensor_tensor(rs[:, 1:2], rs[:, 0:1], neg_half[:, :], ALU.pow).then_inc(att["y_rstd"], 1)
                    z, zn = res[:, kp % 4, 0, :], res[:, kp % 4, 1, :]
                    if phase == 0:
                        wait_apart(pool, pool_passed, att["y_rstd"], p + 1)
                        nc.gpsimd.tensor_scalar(zn, z, mv[:, 0:1], rs[:, 1:2], ALU.subtract, ALU.mult).then_inc(att["y_ready"], 1)
                    else:
                        if kp >= NT + 4:
                            pool.wait_ge(att["tok_done"], p - 3 - NT)
                            pool.wait_ge(moe["tok_kept"], p - 3 - NT)
                        q = p - NT
                        wait_apart(pool, pool_passed, att["y_rstd"], p + 1)
                        nc.gpsimd.tensor_scalar(zn, z, mv[:, 0:1], rs[:, 1:2], ALU.subtract, ALU.mult).then_inc(att["y_norm"], 1)
                        pool.wait_ge(att["y_norm"], q + 1)
                        nc.gpsimd.tensor_tensor(z, zn, ln1[:, 0, :], ALU.mult).then_inc(att["y_gain"], 1)
                        pool.wait_ge(att["y_gain"], q + 1)
                        nc.gpsimd.tensor_tensor(zn, z, ln1[:, 1, :], ALU.add).then_inc(att["y_ready"], 1)

            run_attention(pool, 0, step)
            run_attention(pool, 1, step)

            pool.wait_ge(blanked, 16 * (NT + 1))

            def pack_step(t_, kp, looping):
                p = t_
                wait_apart(pool, pool_passed, moe["tok_copied"], p + 1)
                wait_apart(pool, pool_passed, moe["idx_copied"], p + 1)
                for c in range(TOP):
                    nc.gpsimd.indirect_dma_start(
                        out=packed, out_offset=bass.IndirectOffsetOnAxis(ap=idx_slot[:, kp % 4, c:c + 1], axis=0),
                        in_=tok_slot[:, kp % 4, :], in_offset=None).then_inc(packed_out[kp % 4], 16)

            for n in range(4):
                pack_step(n, n, False)
            with pool.Fori(1, NT // 4) as i:
                for u in range(4):
                    pack_step(i * 4 + u, 4 + u, True)

            def combine_step(t_, k, looping):
                p, kp = t_ + 2, k + 2
                if looping or 0 <= kp < NT:
                    wait_apart(pool, pool_passed, moe["idx_copied"], NT + p + 1)
                    if kp >= 4:
                        wait_apart(pool, pool_passed, moe["z_ready"], p - 3)
                    for c in range(TOP):
                        nc.gpsimd.indirect_dma_start(
                            out=got[:, kp % 4, c, :], out_offset=None, in_=expert_out,
                            in_offset=bass.IndirectOffsetOnAxis(ap=idx_slot[:, kp % 4, c:c + 1], axis=0)).then_inc(got_in[kp % 4], 16)
                p, kp = t_, k
                if looping or 0 <= kp < NT:
                    pool.wait_ge(x1_read[kp % 4], 8 * (p - kp % 4) + 32)
                    nc.gpsimd.tensor_tensor(x1_in[:, kp % 4, :], x1_in[:, kp % 4, :], ln2[:, 1, :], ALU.add).then_inc(moe["x1_added"], 1)
                    mv, rs = mv_b[:, kp % 2, :], rs_b[:, kp % 2, :]
                    wait_apart(pool, pool_passed, moe["x1_added"], p + 1)
                    wait_apart(pool, pool_passed, moe["z_mv"], p + 1)
                    nc.gpsimd.tensor_scalar(rs[:, 0:1], mv[:, 1:2], EPS, None, ALU.add).then_inc(moe["z_var"], 1)
                    pool.wait_ge(moe["z_var"], p + 1)
                    nc.gpsimd.tensor_tensor(rs[:, 1:2], rs[:, 0:1], neg_half[:, :], ALU.pow).then_inc(moe["z_rstd"], 1)

            for n in range(4):
                pool.wait_ge(y_out[n], 16 * NM // 4)
            run_tiles(pool, NT, 1, 3, combine_step)

        @block.vector
        def _(dve):
            nc.vector.memset(zero_tile[:, :], 0.0).then_inc(zero_ready, 1)
            dve.wait_ge(const_in, 16 * CONSTANTS)
            nc.vector.memset(neg_half[:, :], -0.5).then_inc(prep, 1)
            nc.vector.memset(ones[:, :], 1.0).then_inc(zero_ready, 1)
            nc.vector.tensor_scalar(decay[:, :], dist[:, :], td[:, :], -ROOT, ALU.mult, ALU.mult).then_inc(prep, 1)
            nc.vector.tensor_copy(bias_v_wide[:, :, :], bias_v[:, :].unsqueeze(2).broadcast_to([P, 2, P])).then_inc(row_done, 1)
            dve.wait_ge(row_done, 2)
            nc.vector.tensor_tensor(row_add[:, :, :], ps_o[:, 0:2 * D].rearrange("p (a b) -> p a b", a=2), bias_o[:, :, :], ALU.add).then_inc(row_ready, 1)
            dve.wait_ge(prep, 2)
            dve.wait_ge(x_in0, 16)

            def step(t_, k, phase, looping):
                p, kp = t_, k
                here = live(kp, phase, looping)
                sc = ps_s[:, :].rearrange("p (h k) -> p h k", h=H)
                high = neg_max[:, kp % 2, :]
                a = prob[:, kp % 2, :, :]
                if here:
                    dve.wait_ge(att["scores_done"], p + 1)
                    if kp >= 2:
                        dve.wait_ge(att["pt_done"], p - 1)
                        dve.wait_ge(att["shifted"], p - 1)
                    if phase == 0:
                        nc.vector.tensor_tensor(a, sc, decay[:, :].unsqueeze(1).broadcast_to([P, H, S]), ALU.add).then_inc(att["scores_read"], 1)
                    else:
                        nc.vector.tensor_reduce(high, sc, AX.X, ALU.max, negate=True).then_inc(att["max_ready"], 1)
                p2, k2 = t_ - 2, k - 2
                if live(k2, phase, looping):
                    o = ps_o[:, 0:H * (DH + 1)].rearrange("p (h c) -> p h c", h=H)
                    dve.wait_ge(att["pv_done"], p2 + 1)
                    nc.vector.reciprocal(inv_sum[:, k2 % 2, :].unsqueeze(2), o[:, :, DH:DH + 1]).then_inc(att["inv_ready"], 1)
                if here:
                    if phase == 0:
                        dve.wait_ge(att["scores_read"], p + 1)
                        nc.vector.tensor_reduce(high, a, AX.X, ALU.max, negate=True).then_inc(att["max_ready"], 1)
                    else:
                        dve.wait_ge(att["max_ready"], p + 1)
                        nc.vector.tensor_tensor(a, sc, high.unsqueeze(2).broadcast_to([P, H, S]), ALU.add).then_inc(att["shifted"], 1)
                if live(k2, phase, looping):
                    dve.wait_ge(att["inv_ready"], p2 + 1)
                    if k2 >= 2:
                        dve.wait_ge(att["ot_done"], p2 - 1)
                    nc.vector.tensor_tensor(o_sb[:, k2 % 2, :].rearrange("p (h d) -> p h d", h=H), o[:, :, 0:DH],
                                            inv_sum[:, k2 % 2, :].unsqueeze(2).broadcast_to([P, H, DH]), ALU.mult).then_inc(att["o_ready"], 1)
                p, kp = t_ - 6, k - 6
                if phase == 1 and live(kp, phase, looping):
                    q = p - NT
                    dve.wait_ge(att["logits_done"], q + 1)
                    nc.vector.tensor_tensor(logit[:, q, :], ps_o[:, 256:256 + N_EXP], bias_g[:, :], ALU.add).then_inc(att["logits_read"], 1)
                p, kp = t_ + 2, k + 2
                if live(kp, phase, looping):
                    dve.wait_ge(att["proj_done"], p + 1)
                    if kp >= 2:
                        dve.wait_ge(att["scores_done"], p - 1)
                    for n, (dst, mask) in enumerate(((qm, mask_q), (kx, mask_k))):
                        nc.vector.scalar_tensor_tensor(
                            out=dst[:, kp % 2, :, :], in0=ps_qk[:, n * P:n * P + P].unsqueeze(1).broadcast_to([P, G4, P]),
                            scalar=bias_qk[:, phase, n:n + 1], in1=mask[:, :].unsqueeze(2).broadcast_to([P, G4, P]),
                            op0=ALU.add, op1=ALU.mult).then_inc(att["qk_ready"], 1)
                p, kp = t_ + 4, k + 4
                rows_in = phase == 0 and live(kp, phase, looping)
                if rows_in:
                    if kp == 8:
                        dve.wait_ge(x_in1, 16)
                    if kp >= 2:
                        dve.wait_ge(att["xn_ready"], p - 1)
                    nc.vector.bn_stats(stats_a[:, kp % 2, :], x_all[:, p, :]).then_inc(att["x_stats"], 1)
                p2, k2 = t_ - 3, k - 3
                rows_out = live(k2, phase, looping)
                if rows_out:
                    dve.wait_ge(att["y_done"], p2 + 1)
                    dve.wait_ge(att["residual_ready"], p2 + 1)
                    if phase == 0:
                        if k2 >= 4:
                            dve.wait_ge(stored[k2 % 4], 4 * (p2 - k2 % 4))
                    else:
                        dve.wait_ge(att["y_ready"], p2 - 3)
                        dve.wait_ge(stored[k2 % 4], 16 * NT // 4)
                    z = res[:, k2 % 4, 0, :]
                    nc.vector.tensor_tensor(z, ps_y[:, P:2 * P], (x_all, src_all)[phase][:, p2 - phase * NT, :], ALU.add).then_inc(att["y_read"], 1)
                if rows_in:
                    wait_apart(dve, dve_passed, att["x_stats"], p + 1)
                    nc.vector.bn_aggr(mv_a[:, kp % 2, :], stats_a[:, kp % 2, :]).then_inc(att["x_mv"], 1)
                if rows_out:
                    dve.wait_ge(att["y_read"], p2 + 1)
                    if k2 >= 2:
                        dve.wait_ge(att["y_ready"], p2 - 1)
                    nc.vector.bn_stats(stats_b[:, k2 % 2, :], z).then_inc(att["y_stats"], 1)
                    wait_apart(dve, dve_passed, att["y_stats"], p2 + 1)
                    nc.vector.bn_aggr(mv_b[:, k2 % 2, :], stats_b[:, k2 % 2, :]).then_inc(att["y_mv"], 1)
                p3, k3 = t_ - 3, k - 3
                if phase == 0 and live(k3, phase, looping):
                    dve.wait_ge(moe["w_hi_ready"], p3 + 1)
                    part = bass.ds(p3 * W_PART, W_PART)
                    nc.vector.tensor_tensor(w_lo[:, :, :, :].rearrange(flat_w)[:, part], w_given[:, part],
                                            w_hi[:, :, :, :].bitcast(FP32).rearrange(flat_w)[:, part], ALU.subtract).then_inc(moe["w_lo_ready"], 1)
                if rows_in:
                    dve.wait_ge(att["x_rstd"], p + 1)
                    if kp >= 2:
                        dve.wait_ge(att["in_done"], p - 1)
                    nc.vector.tensor_scalar(xn[:, kp % 2, :], x_all[:, p, :], mv_a[:, kp % 2, 0:1], rs_a[:, kp % 2, 1:2],
                                            ALU.subtract, ALU.mult).then_inc(att["xn_ready"], 1)

            run_attention(dve, 0, step)
            run_attention(dve, 1, step)

            made = [0]

            def then(instruction):
                made[0] += 1
                instruction.then_inc(moe["route"], 1)
                dve.wait_ge(moe["route"], made[0])

            dve.wait_ge(const2_in, 16 * (NT + 1))
            dve.wait_ge(att["logits_read"], NT)
            v = nc.vector
            by_expert = rank8[:, :].unsqueeze(1).broadcast_to([P, NT, N_EXP])
            for c in range(TOP):
                left = rest if c else logit
                then(v.tensor_reduce(best[:, c, :], left[:, :, :], AX.X, ALU.max))
                then(v.tensor_tensor(r_key[:, :, :], left[:, :, :], best[:, c, :].unsqueeze(2).broadcast_to([P, NT, N_EXP]), ALU.is_equal))
                then(v.tensor_tensor(r_key[:, :, :], r_key[:, :, :], by_expert, ALU.mult))
                then(v.tensor_reduce(r_top[:, :], r_key[:, :, :], AX.X, ALU.max))
                then(v.tensor_tensor(pick[:, c, :, :], by_expert, r_top[:, :].unsqueeze(2).broadcast_to([P, NT, N_EXP]), ALU.is_equal))
                if c == 0:
                    flat = "p t e -> p (t e)"
                    then(v.scalar_tensor_tensor(out=rest[:, :, :].rearrange(flat), in0=pick[:, 0, :, :].rearrange(flat), scalar=-FAR,
                                                in1=logit[:, :, :].rearrange(flat), op0=ALU.mult, op1=ALU.add))
            then(v.tensor_tensor(both[:, :, :], pick[:, 0, :, :], pick[:, 1, :, :], ALU.add))
            v.tensor_tensor(r_sum[:, :], best[:, 1, :], best[:, 0, :], ALU.subtract).then_inc(moe["route_exp"], 1)
            dve.wait_ge(moe["counted"], 1)
            then(v.tensor_copy(scan[:, 0, :, :].rearrange(flat), ps_y[:, 0:NT * N_EXP]))
            side, gap = 0, 1
            while gap < NT:
                then(v.tensor_copy(scan[:, 1 - side, 0:gap, :], scan[:, side, 0:gap, :]))
                then(v.tensor_tensor(scan[:, 1 - side, gap:, :], scan[:, side, gap:, :], scan[:, side, 0:NT - gap, :], ALU.add))
                side, gap = 1 - side, 2 * gap
            total = scan[:, side, NT - 1, :]
            then(v.tensor_tensor(full[:, :, :], total.unsqueeze(2).broadcast_to([P, N_EXP, NT]),
                                 steps128[:, :].unsqueeze(1).broadcast_to([P, N_EXP, NT]), ALU.is_gt))
            then(v.tensor_reduce(tiles_of[:, :], full[:, :, :], AX.X, ALU.add))
            then(v.tensor_copy(tiles_to[:, 0, :], tiles_of[:, :]))
            at, gap = 0, 1
            while gap < N_EXP:
                then(v.tensor_copy(tiles_to[:, 1 - at, 0:gap], tiles_to[:, at, 0:gap]))
                then(v.tensor_tensor(tiles_to[:, 1 - at, gap:], tiles_to[:, at, gap:], tiles_to[:, at, 0:N_EXP - gap], ALU.add))
                at, gap = 1 - at, 2 * gap
            then(v.tensor_tensor(starts[:, :], tiles_to[:, at, :], tiles_of[:, :], ALU.subtract))
            then(v.tensor_scalar(starts[:, :], starts[:, :], float(P), None, ALU.mult))
            then(v.tensor_tensor(past[:, :, :], tile_no[:, :].unsqueeze(2).broadcast_to([P, NM, N_EXP]),
                                 tiles_to[:, at, :].unsqueeze(1).broadcast_to([P, NM, N_EXP]), ALU.is_ge))
            then(v.tensor_reduce(expert_f[:, :], past[:, :, 0:N_EXP - 1], AX.X, ALU.add))
            then(v.tensor_copy(expert_of[:, :], expert_f[:, :]))
            then(v.tensor_tensor(place[:, :, :].rearrange(flat), scan[:, side, :, :].rearrange(flat), ps_y[:, 0:NT * N_EXP], ALU.subtract))
            then(v.tensor_tensor(place[:, :, :].rearrange(flat), place[:, :, :].rearrange(flat), ps_o[:, 0:NT * N_EXP], ALU.add))
            then(v.tensor_tensor(place[:, :, :], place[:, :, :], starts[:, :].unsqueeze(1).broadcast_to([P, NT, N_EXP]), ALU.add))
            for c in range(TOP):
                then(v.tensor_tensor(r_key[:, :, :], place[:, :, :], pick[:, c, :, :], ALU.mult))
                then(v.tensor_reduce(slot_f[:, c, :], r_key[:, :, :], AX.X, ALU.add))
            then(v.tensor_copy(slot_u[:, :, :], slot_f[:, :, :]))
            dve.wait_ge(moe["route_exp"], 2)
            then(v.tensor_scalar(r_sum[:, :], r_exp[:, :], 1.0, None, ALU.add))
            then(v.reciprocal(share[:, 0, :], r_sum[:, :]))
            then(v.tensor_tensor(share[:, 1, :], share[:, 0, :], r_exp[:, :], ALU.mult))
            dve.wait_ge(moe["tok_kept"], NT)

            def pack_step(t_, kp, looping):
                p = t_
                if kp >= 4:
                    dve.wait_ge(packed_out[kp % 4], 8 * (p - kp % 4))
                v.tensor_copy(tok_slot[:, kp % 4, :], x_all[:, p, :]).then_inc(moe["tok_copied"], 1)
                v.tensor_copy(idx_slot[:, kp % 4, :].unsqueeze(2), slot_u[:, :, bass.ds(p, 1)]).then_inc(moe["idx_copied"], 1)

            for n in range(4):
                pack_step(n, n, False)
            with dve.Fori(1, NT // 4) as i:
                for u in range(4):
                    pack_step(i * 4 + u, 4 + u, True)

            experts = {}

            def expert_step(t_, k, looping):
                load_experts(mybir.EngineType.DVE, t_, k, looping, experts)
                p, kp = t_, k
                if looping or 0 <= kp < NM:
                    e = experts[kp]
                    dve.wait_ge(moe["h_done"], p + 1)
                    if kp >= 2:
                        dve.wait_ge(moe["ht_done"], p - 1)
                    v.tensor_tensor(h_sb[:, kp % 2, :], ps_s[:, F * (kp % 2):F * (kp % 2 + 1)], b1_wide[:, e, :], ALU.add).then_inc(moe["hb_ready"], 1)
                p, kp = t_ + 1, k + 1
                if looping or 0 <= kp < NM:
                    dve.wait_ge(moe["xhi_ready"], p + 1)
                    v.tensor_tensor(x_lo[:, kp % 2, :], ps_in[:, 0:P], x_hi[:, kp % 2, :].bitcast(FP32), ALU.subtract).then_inc(moe["xlo_ready"], 1)
                p, kp = t_ - 1, k - 1
                if looping or 0 <= kp < NM:
                    dve.wait_ge(moe["hhi_ready"], p + 1)
                    v.scalar_tensor_tensor(out=h_lo[:, kp % 2, :], in0=ps_pt[:, F * (kp % 2):F * (kp % 2 + 1)], scalar=0.0,
                                           in1=h_hi[:, kp % 2, :].bitcast(FP32), op0=ALU.max, op1=ALU.subtract).then_inc(moe["hlo_ready"], 1)
                p, kp = t_ - 2, k - 2
                if looping or 0 <= kp < NM:
                    e = experts[kp]
                    dve.wait_ge(moe["yy_done"], p + 1)
                    if kp >= 4:
                        dve.wait_ge(y_out[kp % 4], 4 * (p - kp % 4))
                    v.tensor_tensor(y_sb[:, kp % 4, :], (ps_o, ps_y)[kp % 2][:, 0:D], b2_wide[:, e, :], ALU.add).then_inc(moe["yo_ready"], 1)

            run_tiles(dve, NM, 2, 3, expert_step)

            def combine_step(t_, k, looping):
                p, kp = t_ + 3, k + 3
                if looping or 0 <= kp < NT:
                    if kp >= 4:
                        dve.wait_ge(got_in[kp % 4], 8 * (p - kp % 4))
                    v.tensor_copy(idx_slot[:, kp % 4, :].unsqueeze(2), slot_u[:, :, bass.ds(p, 1)]).then_inc(moe["idx_copied"], 1)
                p, kp = t_, k
                if looping or 0 <= kp < NT:
                    dve.wait_ge(got_in[kp % 4], 8 * (p - kp % 4) + 32)
                    z = z_sb[:, kp % 4, :]
                    v.scalar_tensor_tensor(out=z, in0=got[:, kp % 4, 0, :], scalar=share[:, 0, bass.ds(p, 1)], in1=x_all[:, p, :],
                                           op0=ALU.mult, op1=ALU.add).then_inc(moe["z_part"], 1)
                    dve.wait_ge(moe["z_part"], p + 1)
                    v.scalar_tensor_tensor(out=z, in0=got[:, kp % 4, 1, :], scalar=share[:, 1, bass.ds(p, 1)], in1=z,
                                           op0=ALU.mult, op1=ALU.add).then_inc(moe["z_ready"], 1)
                    dve.wait_ge(moe["z_ready"], p + 1)
                    v.bn_stats(stats_b[:, kp % 2, :], z).then_inc(moe["z_stats"], 1)
                    wait_apart(dve, dve_passed, moe["z_stats"], p + 1)
                    v.bn_aggr(mv_b[:, kp % 2, :], stats_b[:, kp % 2, :]).then_inc(moe["z_mv"], 1)
                p, kp = t_ - 1, k - 1
                if looping or 0 <= kp < NT:
                    z = z_sb[:, kp % 4, :]
                    dve.wait_ge(moe["z_rstd"], p + 1)
                    v.tensor_scalar(z, z, mv_b[:, kp % 2, 0:1], rs_b[:, kp % 2, 1:2], ALU.subtract, ALU.mult).then_inc(moe["z_norm"], 1)
                    dve.wait_ge(moe["z_norm"], p + 1)
                    v.tensor_tensor(z, z, ln2[:, 0, :], ALU.mult).then_inc(moe["z_gain"], 1)
                    dve.wait_ge(moe["z_gain"], p + 1)
                    dve.wait_ge(moe["x1_added"], p + 1)
                    if kp >= 4:
                        dve.wait_ge(out_done[kp % 4], 8 * (p - kp % 4))
                    v.tensor_tensor(o_out[:, kp % 4, :], z, x1_in[:, kp % 4, :], ALU.add).then_inc(moe["o_done"], 1)

            run_tiles(dve, NT, 1, 3, combine_step)

        @block.tensor
        def _(pe):
            pe.wait_ge(const_in, 16 * CONSTANTS)
            pe.wait_ge(weights_in, 16)
            pe.wait_ge(row_done, 1)
            for n in range(2):
                m = nc.tensor.matmul(ps_o[:, n * D:(n + 1) * D], bias_v_wide[:, n, :], w_t[:, 4 * n + 3, :], start=True, stop=True)
            m.then_inc(row_done, 1)

            def step(t_, k, phase, looping):
                p, kp = t_, k
                if live(kp, phase, looping):
                    pe.wait_ge(att["qk_ready"], 2 * p + 2)
                    if kp >= 1:
                        pe.wait_ge(att["shifted"] if phase else att["scores_read"], p)
                    for g in range(G4):
                        for b in range(2):
                            q = slice(64 * b, 64 * b + 64)
                            m = nc.tensor.matmul(ps_s[q, 256 * g:256 * g + 256], qm[:, kp % 2, g, q], kx[:, kp % 2, :, q], start=True, stop=True)
                    m.then_inc(att["scores_done"], 1)
                p, kp = t_ - 5, k - 5
                if phase == 1 and live(kp, phase, looping):
                    pe.wait_ge(att["y_ready"], p + 1)
                    if kp >= NT + 1:
                        pe.wait_ge(att["tok_ready"], p - NT)
                    pe.wait_ge(att["in_ready"], t_ + 3 if looping or k + 2 < 2 * NT else 2 * NT)
                    pe.wait_ge(att["v_ready"], 2 * t_ + 4 if looping or k + 1 < 2 * NT else 4 * NT)
                    nc.tensor.transpose(ps_in[:, 0:P], res[:, kp % 4, 1, :], ident[:, :]).then_inc(att["tok_done"], 1)
                p, kp = t_ - 6, k - 6
                if phase == 1 and live(kp, phase, looping):
                    pe.wait_ge(att["tok_ready"], p + 1 - NT)
                    pe.wait_ge(att["o_ready"], t_ - 2 if looping or k - 3 < 2 * NT else 2 * NT)
                    if kp >= NT + 1:
                        pe.wait_ge(att["logits_read"], p - NT)
                    nc.tensor.matmul(ps_o[:, 256:256 + N_EXP], tok_t[:, kp % 2, :], gate_t[:, :], start=True, stop=True).then_inc(att["logits_done"], 1)
                p, kp = t_ - 2, k - 2
                if live(kp, phase, looping):
                    pe.wait_ge(att["pt_ready"], p + 1)
                    pe.wait_ge(att["v_ready"], 2 * p + 2)
                    if kp >= 1:
                        pe.wait_ge(att["o_ready"], p)
                    if phase == 1 and kp >= NT + 5:
                        pe.wait_ge(att["logits_read"], p - 4 - NT)
                    for h in range(H // 2):
                        for b in range(2):
                            m = nc.tensor.matmul(ps_o[64 * b:64 * b + 64, h * VW:(h + 1) * VW], probt[:, kp % 2, h, 64 * b:64 * b + 64],
                                                 vb[:, kp % 4, b, h, :, :], start=True, stop=True)
                    m.then_inc(att["pv_done"], 1)
                p, kp = t_ + 2, k + 2
                if live(kp, phase, looping):
                    pe.wait_ge(att["in_ready"], p + 1)
                    if kp >= 1:
                        pe.wait_ge(att["qk_ready"], 2 * p)
                        pe.wait_ge(att["v_ready"], 2 * p)
                    if phase == 1 and k - 5 >= NT:
                        pe.wait_ge(att["tok_ready"], t_ - 4 - NT)
                    xt, ct = xct[:, kp % 2, 0, :], xct[:, kp % 2, 1 - phase, :]
                    w = 4 * phase
                    nc.tensor.matmul(ps_qk[:, 0:P], w_t[:, w, :], xt, start=True, stop=True)
                    nc.tensor.matmul(ps_qk[:, P:2 * P], w_t[:, w + 1, :], ct, start=True, stop=True)
                    for b in range(2):
                        for par in range(2):
                            m = nc.tensor.matmul(ps_in[64 * par:64 * par + 64, 256 + P * b:256 + P * b + P], ct[:, 64 * b:64 * b + 64], w_t[:, w + 2, :], start=True, stop=True)
                    m.then_inc(att["proj_done"], 1)
                p, kp = t_ - 3, k - 3
                if live(kp, phase, looping):
                    pe.wait_ge(att["o_ready"], p + 1)
                    if kp >= 1:
                        pe.wait_ge(att["y_read"], p)
                    nc.tensor.transpose(ps_y[:, 0:P], o_sb[:, kp % 2, :], ident[:, :]).then_inc(att["ot_done"], 1)
                p, kp = t_ - 1, k - 1
                if live(kp, phase, looping):
                    pe.wait_ge(att["probs_ready"], p + 1)
                    if kp >= 1:
                        pe.wait_ge(att["pt_ready"], p)
                    for h in range(H // 2):
                        m = nc.tensor.transpose(ps_pt[:, h * P:(h + 1) * P], prob[:, kp % 2, 2 * h:2 * h + 2, :], ident[:, :])
                    m.then_inc(att["pt_done"], 1)
                p, kp = t_ + 3, k + 3
                if live(kp, phase, looping):
                    pe.wait_ge(att["xn_ready"], p + 1)
                    if kp >= 1:
                        pe.wait_ge(att["v_ready"], 2 * p)
                        pe.wait_ge(att["in_ready"], p)
                    if phase == 0:
                        pe.wait_ge(ctx_ready[kp % 4], 4 * (p - kp % 4) + 16)
                        nc.tensor.transpose(ps_in[:, P:2 * P], ctx_in[:, kp % 4, :], ident[:, :])
                    nc.tensor.transpose(ps_in[:, 0:P], xn[:, kp % 2, :], ident[:, :]).then_inc(att["in_done"], 1)
                p, kp = t_ - 3, k - 3
                if live(kp, phase, looping):
                    pe.wait_ge(att["ot_ready"], p + 1)
                    nc.tensor.matmul(ps_y[:, P:2 * P], ot_sb[:, kp % 2, :], w_t[:, 4 * phase + 3, :], start=True, stop=True).then_inc(att["y_done"], 1)

            run_attention(pe, 0, step)
            run_attention(pe, 1, step)

            pe.wait_ge(const2_in, 16 * (NT + 1))
            pe.wait_ge(zero_ready, 2)
            pe.wait_ge(moe["route"], 12)
            picked = both[:, :, :].rearrange("p t e -> p (t e)")
            nc.tensor.matmul(ps_o[:, 0:NT * N_EXP], earlier[:, :], picked, start=True, stop=True)
            nc.tensor.matmul(ps_y[:, 0:NT * N_EXP], ones[:, :], picked, start=True, stop=True).then_inc(moe["counted"], 1)
            pe.wait_ge(moe["idx_copied"], 1)

            experts = {}

            def expert_step(t_, k, looping):
                load_experts(mybir.EngineType.PE, t_, k, looping, experts)
                p, kp = t_, k
                if looping or 0 <= kp < NM:
                    e = experts[kp]
                    pe.wait_ge(moe["xlo_ready"], p + 1)
                    if kp >= 2:
                        pe.wait_ge(moe["hb_ready"], p - 1)
                    a = ps_s[:, F * (kp % 2):F * (kp % 2 + 1)]
                    nc.tensor.matmul(a, x_lo[:, kp % 2, :], w_hi[:, 0, e, :], start=True, stop=False)
                    nc.tensor.matmul(a, x_hi[:, kp % 2, :], w_lo[:, 0, e, :], start=False, stop=False)
                    nc.tensor.matmul(a, x_hi[:, kp % 2, :], w_hi[:, 0, e, :], start=False, stop=True).then_inc(moe["h_done"], 1)
                p, kp = t_ + 1, k + 1
                if looping or 0 <= kp < NM:
                    pe.wait_ge(xs_in[kp % 4], 4 * (p - kp % 4) + 16)
                    if kp >= 1:
                        pe.wait_ge(moe["xlo_ready"], p)
                    nc.tensor.transpose(ps_in[:, 0:P], xs[:, kp % 4, :], ident[:, :]).then_inc(moe["xt_done"], 1)
                p, kp = t_ - 1, k - 1
                if looping or 0 <= kp < NM:
                    pe.wait_ge(moe["hb_ready"], p + 1)
                    if kp >= 2:
                        pe.wait_ge(moe["hlo_ready"], p - 1)
                    for c in range(FC):
                        m = nc.tensor.transpose(ps_pt[:, F * (kp % 2) + c * P:F * (kp % 2) + (c + 1) * P], h_sb[:, kp % 2, c * P:(c + 1) * P], ident[:, :])
                    m.then_inc(moe["ht_done"], 1)
                p, kp = t_ - 2, k - 2
                if looping or 0 <= kp < NM:
                    e = experts[kp]
                    pe.wait_ge(moe["hlo_ready"], p + 1)
                    if kp >= 2:
                        pe.wait_ge(moe["yo_ready"], p - 1)
                    a = (ps_o, ps_y)[kp % 2][:, 0:D]
                    n = 0
                    for h, w in ((h_lo, w_hi), (h_hi, w_lo), (h_hi, w_hi)):
                        for c in range(FC):
                            m = nc.tensor.matmul(a, h[:, kp % 2, c * P:(c + 1) * P], w[:, 1, e, c * P:(c + 1) * P], start=n == 0, stop=n == 3 * FC - 1)
                            n += 1
                    m.then_inc(moe["yy_done"], 1)

            run_tiles(pe, NM, 2, 3, expert_step)


_SHORT = {"x": "x", "ctx_1024": "ctx"}


def kernel(**inputs):
    import numpy as _np
    import concourse.bacc as _bacc
    from concourse import mybir as _mybir
    from concourse.bass_utils import run_bass_kernel_spmd as _run

    nc = _bacc.Bacc("TRN2", target_bir_lowering=False, num_devices=1)
    arrays, t = {}, {}
    part = _np.arange(P)
    columns = (
        _np.eye(P), _np.abs(part[:, None] % S - _np.arange(S)), part[:, None] // 32 == _np.arange(G4),
        part[:, None] // DH % G4 == _np.arange(G4), part[:, None] < part, _np.tile(N_EXP - _np.arange(N_EXP), (P, 1)),
        _np.tile(_np.arange(NT) * P, (P, 1)), _np.tile(_np.arange(NM), (P, 1)))
    given = {_SHORT.get(n, n.replace("L0_xattn_", "").replace("L0_ffn_", "")): _np.asarray(a) for n, a in inputs.items()}
    in_b = given["in_proj_b"]
    laid = {
        "shapes": _np.concatenate(columns, axis=1, dtype=_np.float32),
        "weights": _np.stack([given[n].T for n in ("wq", "wk", "wv", "wo")] + [a.T for a in given["in_proj_w"].reshape(3, D, D)] + [given["out_w"].T], axis=1),
        "gate_w": given["gate_w"].T,
        "expert_w": _np.concatenate([given["w1"].transpose(2, 0, 1).reshape(P, N_EXP * F),
                                     given["w2"].reshape(N_EXP, D, FC, P).transpose(3, 0, 2, 1).reshape(P, N_EXP * F)], axis=1),
        "columns": _np.stack([given["bq"], given["bk"], in_b[0:D], in_b[D:2 * D], given["bv"], in_b[2 * D:]], axis=1),
        "rows": _np.stack([given[n] for n in ("bo", "out_b", "ln1_g", "ln1_b", "ln2_g", "ln2_b")]),
        "time_decay": given["time_decay"].reshape(1, 1),
    }
    for name in ("x", "ctx", "gate_b", "b1", "b2"):
        laid[name] = given[name]
    for name, a in laid.items():
        a = _np.ascontiguousarray(a)
        arrays[f"in_{name}"] = a
        t[name] = nc.dram_tensor(f"in_{name}", a.shape, _mybir.dt.from_np(a.dtype), kind="ExternalInput").ap()
    out = nc.dram_tensor("out_0", (B, S, D), FP32, kind="ExternalOutput").ap()
    scratch = nc.dram_tensor("scratch", (B * S, 2, D), FP32).ap()
    packed = nc.dram_tensor("packed", (NM * P, D), FP32).ap()
    expert_out = nc.dram_tensor("expert_out", (NM * P, D), FP32).ap()
    build(nc, t, out, scratch, packed, expert_out)
    r = _run(nc, [arrays], core_ids=[0])
    return r.results[0]["out_0"]
```

```python
import concourse.bass as bass
from concourse import mybir
from contextlib import ExitStack

FP32 = mybir.dt.float32
FP32R = mybir.dt.float32r
BF16 = mybir.dt.bfloat16
UINT32 = mybir.dt.uint32
INT32 = mybir.dt.int32
ALU = mybir.AluOpType
ACT = mybir.ActivationFunctionType
AX = mybir.AxisListType

B, S, D = 64, 64, 128
H = 16
DH = D // H
P = 128
NT = B * S // P
G4 = 4
VW = 2 * (DH + 1)
EPS = 1e-5
ROOT = float(DH) ** 0.5
N_EXP, F = 8, 512
FC = F // P
TOP = 2
COMBINE = 4
W_PART = 2 * N_EXP * F // NT
NM = (TOP * B * S + N_EXP * (P - 1)) // P
NM += -NM % 4
SPARE = NM - TOP * B * S // P
REGION = B * S + P
ROUTE = 20
FAR = 3.0e38
WIDTHS = (P, S, G4, G4, P, N_EXP, N_EXP, NT, NM, TOP * NT, NM)
SHAPES = [(sum(WIDTHS[:n]), sum(WIDTHS[:n + 1])) for n in range(len(WIDTHS))]
SHAPES_END = sum(WIDTHS)


def build(nc, t, out, scratch, packed, results):
    ctx = ExitStack()
    with ctx:
        def sb(name, shape, dt=FP32):
            return ctx.enter_context(nc.sbuf_tensor(name, shape, dt))

        def ps(name, cols):
            return ctx.enter_context(nc.psum_tensor(name, [P, cols], FP32))

        def sem(name):
            return ctx.enter_context(nc.semaphore(name))

        shapes = sb("shapes", [P, SHAPES_END])
        ident, dist, mask_q, mask_k, earlier, rank8, region_at, steps128, tile_no, result_at, padding_at = (
            shapes[:, a:b] for a, b in SHAPES)
        neg_half = sb("neg_half", [P, 1])
        decay = sb("decay", [P, S])
        td = sb("td", [P, 1])
        w_t = sb("w_t", [P, 8, D])
        gate_t = sb("gate_t", [P, N_EXP])
        columns = sb("columns", [P, 6])
        bias_qk = columns[:, 0:4].rearrange("p (a b) -> p a b", a=2)
        bias_v = columns[:, 4:6]
        rows = sb("rows", [P, 6, D])
        bias_o, ln1, ln2 = rows[:, 0:2, :], rows[:, 2:4, :], rows[:, 4:6, :]
        bias_v_wide = sb("bias_v_wide", [P, 2, P])
        bias_g = sb("bias_g", [P, N_EXP])
        row_add = sb("row_add", [P, 2, D])
        w_split = sb("w_split", [P, 2 * N_EXP * FC, 2, P], FP32R)
        w1_split, w2_split = (w_split[:, n * N_EXP * FC:(n + 1) * N_EXP * FC, :, :].rearrange("p (e c) s f -> p e c s f", e=N_EXP) for n in (0, 1))
        b1_wide = sb("b1_wide", [P, N_EXP, F])
        b2_wide = sb("b2_wide", [P, N_EXP, D])
        zero_tile = sb("zero_tile", [P, D + 1])
        ones = sb("ones", [P, P], BF16)
        earlier_b = sb("earlier_b", [P, P], BF16)
        x_all = sb("x_all", [P, NT, D])
        src_all = sb("src_all", [P, NT, D])
        ctx_in = sb("ctx_in", [P, 4, D])
        xn = sb("xn", [P, 2, D])
        xct = sb("xct", [P, 2, 2, D])
        qm = sb("qm", [P, 2, G4, P])
        kx = sb("kx", [P, 2, G4, P])
        vb = sb("vb", [P, 4, 2, H // 2, 2, DH + 1])
        prob = sb("prob", [P, 2, H, S])
        probt = sb("probt", [P, 2, H // 2, P])
        neg_max = sb("neg_max", [P, 2, H])
        inv_sum = sb("inv_sum", [P, 2, H])
        o_sb = sb("o_sb", [P, 2, D])
        ot_sb = sb("ot_sb", [P, 2, D])
        stats_a = sb("stats_a", [P, 2, 6])
        mv_a = sb("mv_a", [P, 2, 2])
        rs_a = sb("rs_a", [P, 2, 2])
        stats_b = sb("stats_b", [P, 2, 6])
        mv_b = sb("mv_b", [P, 2, 2])
        rs_b = sb("rs_b", [P, 2, 2])
        res = sb("res", [P, 4, 2, D])
        tok_t = sb("tok_t", [P, 2, P])
        logit = sb("logit", [P, NT, N_EXP])
        with ExitStack() as early:
            w_given = early.enter_context(nc.sbuf_tensor("w_given", [P, 2 * N_EXP * F], FP32))
        best = sb("best", [P, TOP, NT])
        pick = sb("pick", [P, TOP, NT, N_EXP])
        r_key = sb("r_key", [P, TOP, NT, N_EXP])
        r_top = sb("r_top", [P, NT])
        rest = sb("rest", [P, NT, N_EXP])
        both = sb("both", [P, NT, N_EXP], BF16)
        running = sb("running", [P, N_EXP])
        place = sb("place", [P, NT, N_EXP])
        slot_f = sb("slot_f", [P, TOP, NT])
        slot_u = sb("slot_u", [P, TOP, NT], UINT32)
        share = sb("share", [P, TOP, NT])
        r_exp = sb("r_exp", [P, NT])
        r_sum = sb("r_sum", [P, NT])
        full = sb("full", [P, N_EXP, NT])
        tiles_of = sb("tiles_of", [P, N_EXP])
        tiles_to = sb("tiles_to", [P, 2, N_EXP])
        filled = sb("filled", [P, N_EXP])
        ends = sb("ends", [P, N_EXP], INT32)
        past = sb("past", [P, NM, N_EXP])
        expert_f = sb("expert_f", [P, NM])
        expert_of = sb("expert_of", [P, NM], INT32)
        row_f = sb("row_f", [P, NM])
        row_of = sb("row_of", [P, NM], INT32)
        tok_slot = sb("tok_slot", [P, 4, TOP, D + 1])
        idx_slot = sb("idx_slot", [P, 4, TOP], UINT32)
        xs = sb("xs", [P, 4, D + 1])
        xs_place = sb("xs_place", [P, 4, 1], UINT32)
        x_hi = sb("x_hi", [P, 2, P], FP32R)
        x_lo = sb("x_lo", [P, 2, P], FP32R)
        h_hi = sb("h_hi", [P, 2, F], FP32R)
        h_lo = sb("h_lo", [P, 2, F], FP32R)
        stats_z = sb("stats_z", [P, 2, COMBINE, 6])
        mv_z = sb("mv_z", [P, 2, COMBINE, 2])
        rs_z = sb("rs_z", [P, 2, COMBINE, 3])

        flat_a = prob[:, :, :, :].rearrange("p s h k -> p (s h k)")
        flat_b = probt[:, :, :, :].rearrange("p s h q -> p (s h q)")
        got = [half[:, n * TOP * COMBINE * D:(n + 1) * TOP * COMBINE * D].rearrange("p (c n d) -> p c n d", c=TOP, n=COMBINE)
               for half in (flat_a, flat_b) for n in (0, 1)]
        h_sb = flat_b[:, 0:2 * F].rearrange("p (s f) -> p s f", s=2)
        y_sb = flat_b[:, 8 * D:12 * D].rearrange("p (s d) -> p s d", s=4)

        ps_in = ps("ps_in", 512)
        ps_qk = ps("ps_qk", 512)
        ps_s = ps("ps_s", 1024)
        ps_pt = ps("ps_pt", 1024)
        ps_o = ps("ps_o", 512)
        ps_y = ps("ps_y", 512)

        const2_in = sem("const2_in")
        weights_in, const_in, x_in0, x_in1 = sem("weights_in"), sem("const_in"), sem("x_in0"), sem("x_in1")
        src_in = [sem(f"src_in{n}") for n in range(4)]
        zeroed, row_done, prep = sem("zeroed"), sem("row_done"), sem("prep")
        row_ready = sem("row_ready")
        ctx_ready = [sem(f"ctx_ready{n}") for n in range(4)]
        stored = [sem(f"stored{n}") for n in range(4)]
        names = ("x_stats x_mv x_var x_rstd xn_ready residual_ready in_done in_ready proj_done qk_ready "
                 "v_ready scores_done scores_read max_ready shifted probs_ready pt_done pt_ready pv_done "
                 "inv_ready o_ready ot_done ot_ready y_done y_read y_stats y_mv y_var y_rstd y_norm y_gain "
                 "y_ready tok_done tok_ready logits_done logits_read").split()
        att = {n: sem(n) for n in names}
        names = ("w_hi_ready w_lo_ready counted route_exp route tiles_known "
                 "xt_done xhi_ready xlo_ready h_done hb_ready ht_done hhi_ready hlo_ready yy_done yo_ready "
                 "yb_ready place_ready tok_copied idx_copied x1_added z_part z_ready z_stats z_mv z_var z_rstd z_shift z_norm z_gain o_done last_gain last_done tok_kept").split()
        moe = {n: sem(n) for n in names}
        blanked, zero_ready = sem("blanked"), sem("zero_ready")
        expert_w_in = [sem(f"expert_w_in{n}") for n in range(4)]
        packed_out = [sem(f"packed_out{n}") for n in range(4)]
        xs_in = [sem(f"xs_in{n}") for n in range(4)]
        y_out = [sem(f"y_out{n}") for n in range(4)]
        got_in = [sem(f"got_in{n}") for n in range(4)]
        x1_read = [sem(f"x1_read{n}") for n in range(4)]
        out_done = sem("out_done")
        dve_passed, pool_passed = sem("dve_passed"), sem("pool_passed")

        CONSTANTS = 6

        block = ctx.enter_context(nc.Block())

        def run_attention(eng, phase, step):
            first = phase * NT
            peeled = 16 if phase else 8
            for n in range(-4, peeled):
                step(first + n, first + n, phase, False)
            with eng.Fori(peeled // 4, NT // 4 - 1) as i:
                for u in range(4):
                    step(i * 4 + (first + u), first + peeled + u, phase, True)
            for n in range(NT - 4, NT + (12 if phase else 6)):
                step(first + n, first + n, phase, False)

        def run_tiles(eng, count, behind, ahead, step):
            for n in range(-ahead, 8):
                step(n, n, False)
            with eng.Fori(2, count // 4 - 1) as i:
                for u in range(4):
                    step(i * 4 + u, 8 + u, True)
            for n in range(count - 4, count + behind):
                step(n, n, False)

        def wait_apart(eng, passed, semaphore, value):
            eng.wait_ge(semaphore, value)
            eng.sem_inc(passed, 1)

        def load_values(engine, table, first, count, most, why):
            _, values = nc.values_load_multi_w_load_instructions(
                table[0:1, bass.ds(first, count)], [engine], min_val=0, max_val=most, skip_runtime_bounds_check_because=why)
            return values

        def load_experts(engine, t_, k, looping, experts):
            if k % 4 == 0 if looping else k in (0, NM - 4):
                behind = 2 if k else 0
                values = load_values(engine, expert_of, t_ - behind, 6 if k else 8, N_EXP - 1,
                                     "experts' numbers are counts of at most N_EXP - 1 terms that are 0 or 1")
                experts.update((k - behind + n, value) for n, value in enumerate(values))

        def live(k, phase, looping):
            return looping or 0 <= k - phase * NT < NT

        @block.sync
        def _(sp):
            sp.dma_start(shapes[:, :], t["shapes"]).then_inc(const_in, 16)
            sp.dma_start(w_t[:, :, :], t["weights"]).then_inc(weights_in, 16)
            x_v = t["x"].rearrange("b s d -> (b s) d").rearrange("(n p) d -> p n d", p=P)
            c_v = t["ctx"].rearrange("b s d -> (b s) d")
            b1_v = t["b1"].rearrange("e f -> (e f)")

            def step(t_, k, phase, looping):
                p, kp = t_ + 4, k + 4
                if phase == 0 and live(kp, phase, looping):
                    if kp >= 4:
                        sp.wait_ge(att["in_done"], p - 3)
                    sp.dma_start(ctx_in[:, kp % 4, :], c_v[bass.ds(p * P, P), :]).then_inc(ctx_ready[kp % 4], 16)
                p, kp = t_ - 3, k - 3
                if phase == 0 and live(kp, phase, looping):
                    sp.wait_ge(att["y_ready"], p + 1)
                    sp.dma_start(scratch[bass.ds(p * P, P), :, :], res[:, kp % 4, :, :]).then_inc(stored[kp % 4], 16)
                p, kp = t_, k
                if phase == 0 and live(kp, phase, looping):
                    if kp == 0:
                        sp.dma_start(x_all[:, 8:NT, :], x_v[:, 8:NT, :]).then_inc(x_in1, 16)
                        sp.wait_ge(zero_ready, 1)
                        sp.dma_start(packed[N_EXP * REGION:, :].rearrange("(n p) d -> p n d", p=P),
                                     zero_tile[:, :].unsqueeze(1).broadcast_to([P, SPARE, D + 1])).then_inc(blanked, 16)
                    sp.dma_start(w_given[:, bass.ds(p * W_PART, W_PART)], t["expert_w"][:, bass.ds(p * W_PART, W_PART)]).then_inc(expert_w_in[kp % 4], 16)
                    sp.dma_start(b1_wide[:, :, :].rearrange("p e f -> p (e f)")[:, bass.ds(p * P, P)],
                                 b1_v[bass.ds(p * P, P)].unsqueeze(0).broadcast_to([P, P])).then_inc(const2_in, 16)

            run_attention(sp, 0, step)
            for n in range(4):
                sp.wait_ge(stored[n], 16 * NT // 4)
            s_v = scratch.rearrange("(i r c) a d -> c i r a d", i=B, c=2)
            for n in range(4):
                for c in range(2):
                    sp.dma_start(src_all[c * 64:c * 64 + 64, 8 * n:8 * n + 8, :], s_v[c, :, 8 * n:8 * n + 8, 1, :]).then_inc(src_in[n], 16)

            sp.wait_ge(att["y_read"], 2 * NT)
            for n in range(4):
                for c in range(2):
                    sp.dma_start(src_all[c * 64:c * 64 + 64, 8 * n:8 * n + 8, :], s_v[c, :, 8 * n:8 * n + 8, 0, :]).then_inc(x1_read[n], 16)

            sp.wait_ge(moe["tiles_known"], 1)
            row_range = "rows are sums of counts of tokens and tiles and stay within the packed tensor"
            after = load_values(mybir.EngineType.SP, ends, 0, N_EXP, N_EXP * REGION, row_range)
            for e in range(N_EXP):
                sp.dma_start(packed[bass.ds(after[e], P), :], zero_tile[:, :]).then_inc(blanked, 16)
            for n in range(4):
                sp.wait_ge(packed_out[n], 2 * 16 * NT // 4)
            sp.wait_ge(blanked, 16 * (1 + N_EXP))
            row = {}

            def expert_step(t_, k, looping):
                p, kp = t_ + 3, k + 3
                if looping or 0 <= kp < NM:
                    if k % 4 == 0 if looping else kp in (0, 8, NM - 1):
                        count = 4 if looping else {0: 8, 8: 3, NM - 1: 1}[kp]
                        values = load_values(mybir.EngineType.SP, row_of, p, count, (N_EXP * REGION + SPARE * P) - P, row_range)
                        row.update((kp + n, value) for n, value in enumerate(values))
                    if kp >= 4:
                        sp.wait_ge(moe["xt_done"], p - 3)
                        sp.wait_ge(moe["place_ready"], p - 3)
                    sp.dma_start(xs[:, kp % 4, :], packed[bass.ds(row[kp], P), :]).then_inc(xs_in[kp % 4], 16)

            run_tiles(sp, NM, 2, 3, expert_step)

            for n in range(4):
                sp.wait_ge(y_out[n], 16 * NM // 4)
            r_v = results[NM * P:, :].rearrange("(c n p) d -> p c n d", c=TOP, p=P)
            out_v = out.rearrange("i (r c) d -> c i r d", c=2)

            def results_in(g):
                for c in range(TOP):
                    sp.dma_start(got[g % 4][:, c, :, :], r_v[:, c, g * COMBINE:(g + 1) * COMBINE, :]).then_inc(got_in[g % 4], 16)

            for g in range(4):
                results_in(g)
            for g in range(NT // COMBINE):
                if g + 4 < NT // COMBINE:
                    sp.wait_ge(moe["z_ready"], COMBINE * (g + 1))
                    results_in(g + 4)
                if g < NT // COMBINE - 1:
                    sp.wait_ge(moe["o_done"], g + 1)
                else:
                    sp.wait_ge(moe["last_done"], 1)
                for c in range(2):
                    sp.dma_start(out_v[c, :, g * COMBINE:(g + 1) * COMBINE, :],
                                 x_all[64 * c:64 * c + 64, g * COMBINE:(g + 1) * COMBINE, :]).then_inc(out_done, 16)
            sp.wait_ge(out_done, 2 * 16 * NT // COMBINE)

        @block.scalar
        def _(act):
            act.dma_start(x_all[:, 0:8, :], t["x"].rearrange("b s d -> (b s) d").rearrange("(n p) d -> p n d", p=P)[:, 0:8, :]).then_inc(x_in0, 16)
            act.dma_start(columns[:, :], t["columns"]).then_inc(const_in, 16)
            act.dma_start(td[:, :], t["time_decay"].broadcast_to([P, 1])).then_inc(const_in, 16)
            act.dma_start(rows[:, :, :], t["rows"].unsqueeze(0).broadcast_to([P, 6, D])).then_inc(const_in, 16)
            act.dma_start(bias_g[:, :], t["gate_b"].unsqueeze(0).broadcast_to([P, N_EXP])).then_inc(const_in, 16)
            act.dma_start(gate_t[:, :], t["gate_w"]).then_inc(const_in, 16)
            act.dma_start(b2_wide[:, :, :], t["b2"].unsqueeze(0).broadcast_to([P, N_EXP, D])).then_inc(const2_in, 16)

            def step(t_, k, phase, looping):
                p, kp = t_ - 1, k - 1
                if live(kp, phase, looping):
                    act.wait_ge(att["shifted"], p + 1)
                    a = prob[:, kp % 2, :, :].rearrange("p h k -> p (h k)")
                    nc.scalar.activation(a, a, ACT.Exp, scale=1.0 / ROOT).then_inc(att["probs_ready"], 1)
                p, kp = t_ - 5, k - 5
                if phase == 1 and live(kp, phase, looping):
                    act.wait_ge(att["tok_done"], p + 1 - NT)
                    if kp >= NT + 2:
                        act.wait_ge(att["logits_done"], p - 1 - NT)
                    nc.scalar.activation(tok_t[:, kp % 2, :], ps_in[:, 0:P], ACT.Copy).then_inc(att["tok_ready"], 1)
                    act.wait_ge(att["y_ready"], p + 1)
                    nc.scalar.activation(x_all[:, p - NT, :], res[:, kp % 4, 1, :], ACT.Copy).then_inc(moe["tok_kept"], 1)
                p, kp = t_ + 2, k + 2
                if live(kp, phase, looping):
                    act.wait_ge(att["proj_done"], p + 1)
                    if kp >= 4:
                        act.wait_ge(att["pv_done"], p - 3)
                    else:
                        act.wait_ge(zeroed, 3)
                    for par in range(2):
                        nc.scalar.activation(
                            vb[64 * par:64 * par + 64, kp % 4, :, :, par, 0:DH],
                            ps_in[64 * par:64 * par + 64, 256:512].rearrange("p (b h e d) -> p b h e d", b=2, e=2, d=DH)[:, :, :, par, :],
                            ACT.Copy).then_inc(att["v_ready"], 1)
                p, kp = t_ - 3, k - 3
                if live(kp, phase, looping):
                    act.wait_ge(att["ot_done"], p + 1)
                    if kp >= 2:
                        act.wait_ge(att["y_done"], p - 1)
                    nc.scalar.activation(ot_sb[:, kp % 2, :], ps_y[:, 0:D], ACT.Copy).then_inc(att["ot_ready"], 1)
                p, kp = t_ - 1, k - 1
                if live(kp, phase, looping):
                    act.wait_ge(att["pt_done"], p + 1)
                    if kp >= 2:
                        act.wait_ge(att["pv_done"], p - 1)
                    nc.scalar.activation(probt[:, kp % 2, :, :].rearrange("p h q -> p (h q)"), ps_pt[:, :], ACT.Copy).then_inc(att["pt_ready"], 1)
                p, kp = t_ + 3, k + 3
                if live(kp, phase, looping):
                    act.wait_ge(att["in_done"], p + 1)
                    if kp >= 2:
                        act.wait_ge(att["proj_done"], p - 1)
                    n = 2 - phase
                    nc.scalar.activation(xct[:, kp % 2, 0:n, :].rearrange("p a b -> p (a b)"), ps_in[:, 0:n * D], ACT.Copy).then_inc(att["in_ready"], 1)
                p, kp = t_ + 4, k + 4
                if phase == 1 and live(kp, phase, looping):
                    if kp % (4 if looping else 8) == 0:
                        for n in range(4) if looping else [(kp - NT) // 8]:
                            act.wait_ge(src_in[n], 32)
                    act.wait_ge(att["in_done"], p - 1)
                    nc.scalar.activation(xn[:, kp % 2, :], src_all[:, p - NT, :], ACT.Copy).then_inc(att["xn_ready"], 1)
                q, kq = t_ - 12 - NT, k - 12 - NT
                if phase == 1 and (looping or 0 <= kq < NT):
                    if kq >= 4:
                        act.wait_ge(packed_out[kq % 4], 8 * (q - kq % 4))
                    act.wait_ge(moe["route"], (q - kq % 4) * (ROUTE // 4) + ROUTE)
                    nc.scalar.activation(idx_slot[:, kq % 4, :].unsqueeze(2), slot_u[:, :, bass.ds(q, 1)], ACT.Copy).then_inc(moe["idx_copied"], 1)
                    act.wait_ge(moe["tok_kept"], q + 1)
                    nc.scalar.activation(tok_slot[:, kq % 4, :, 0:D], x_all[:, bass.ds(q, 1), :].broadcast_to([P, TOP, D]), ACT.Copy).then_inc(moe["tok_copied"], 1)
                    nc.scalar.activation(tok_slot[:, kq % 4, :, D:D + 1], result_at.rearrange("p (c n) -> p c n", c=TOP)[:, :, bass.ds(q, 1)], ACT.Copy).then_inc(moe["tok_copied"], 1)
                p, kp = t_ - 2, k - 2
                if phase == 0 and live(kp, phase, looping):
                    act.wait_ge(expert_w_in[kp % 4], 4 * (p - kp % 4) + 16)
                    nc.scalar.activation(w_split[:, bass.ds(p * (W_PART // P), W_PART // P), 0, :],
                                         w_given[:, bass.ds(p * W_PART, W_PART)].rearrange("p (c f) -> p c f", f=P), ACT.Copy).then_inc(moe["w_hi_ready"], 1)

            run_attention(act, 0, step)
            act.wait_ge(moe["w_lo_ready"], NT)
            run_attention(act, 1, step)

            act.wait_ge(moe["route_exp"], 1)
            nc.scalar.activation(r_exp[:, :], r_sum[:, :], ACT.Exp).then_inc(moe["route_exp"], 1)

            def expert_step(t_, k, looping):
                p, kp = t_ + 1, k + 1
                if looping or 0 <= kp < NM:
                    act.wait_ge(moe["xt_done"], p + 1)
                    if kp >= 2:
                        act.wait_ge(moe["h_done"], p - 1)
                    nc.scalar.activation(x_hi[:, kp % 2, :], ps_in[:, 0:P], ACT.Copy).then_inc(moe["xhi_ready"], 1)
                p, kp = t_ - 1, k - 1
                if looping or 0 <= kp < NM:
                    act.wait_ge(moe["ht_done"], p + 1)
                    if kp >= 2:
                        act.wait_ge(moe["yy_done"], p - 1)
                    nc.scalar.activation(h_hi[:, kp % 2, :], ps_pt[:, F * (kp % 2):F * (kp % 2 + 1)], ACT.Relu).then_inc(moe["hhi_ready"], 1)

            run_tiles(act, NM, 2, 3, expert_step)

            for g in range(NT // COMBINE):
                act.wait_ge(moe["z_shift"], g + 1)
                for n in range(COMBINE):
                    z = x_all[:, g * COMBINE + n, :]
                    rs = rs_z[:, g % 2, n, :]
                    nc.scalar.activation(z, z, ACT.Identity, bias=rs[:, 2:3], scale=rs[:, 1:2]).then_inc(moe["z_norm"], 1)

        @block.gpsimd
        def _(pool):
            pool.memset(vb[:, :, :, :, :, :].rearrange("p s b h e d -> p (s b h e d)"), 0.0).then_inc(zeroed, 1)
            for par in range(2):
                pool.wait_ge(zeroed, par + 1)
                pool.memset(vb[64 * par:64 * par + 64, :, :, :, par, DH:DH + 1], 1.0).then_inc(zeroed, 1)
            pool.wait_ge(zeroed, 3)
            pool.wait_ge(prep, 2)
            pool.wait_ge(row_ready, 1)

            def step(t_, k, phase, looping):
                p, kp = t_, k
                if phase == 0 and live(kp, phase, looping):
                    pool.wait_ge(att["max_ready"], p + 1)
                    a = prob[:, kp % 2, :, :]
                    nc.gpsimd.tensor_tensor(a, a, neg_max[:, kp % 2, :].unsqueeze(2).broadcast_to([P, H, S]), ALU.add).then_inc(att["shifted"], 1)
                p, kp = t_ + 4, k + 4
                if phase == 0 and live(kp, phase, looping):
                    mv, rs = mv_a[:, kp % 2, :], rs_a[:, kp % 2, :]
                    wait_apart(pool, pool_passed, att["x_mv"], p + 1)
                    nc.gpsimd.tensor_scalar(rs[:, 0:1], mv[:, 1:2], EPS, None, ALU.add).then_inc(att["x_var"], 1)
                    pool.wait_ge(att["x_var"], p + 1)
                    nc.gpsimd.tensor_tensor(rs[:, 1:2], rs[:, 0:1], neg_half[:, :], ALU.pow).then_inc(att["x_rstd"], 1)
                p, kp = t_ - 2, k - 2
                if live(kp, phase, looping):
                    a = (x_all, src_all)[phase][:, p - phase * NT, :]
                    pool.wait_ge(att["xn_ready"], p + 1)
                    nc.gpsimd.tensor_tensor(a, a, row_add[:, phase, :], ALU.add).then_inc(att["residual_ready"], 1)
                p, kp = t_ - 3, k - 3
                if live(kp, phase, looping):
                    mv, rs = mv_b[:, kp % 2, :], rs_b[:, kp % 2, :]
                    wait_apart(pool, pool_passed, att["y_mv"], p + 1)
                    nc.gpsimd.tensor_scalar(rs[:, 0:1], mv[:, 1:2], EPS, None, ALU.add).then_inc(att["y_var"], 1)
                    pool.wait_ge(att["y_var"], p + 1)
                    nc.gpsimd.tensor_tensor(rs[:, 1:2], rs[:, 0:1], neg_half[:, :], ALU.pow).then_inc(att["y_rstd"], 1)
                    z, zn = res[:, kp % 4, 0, :], res[:, kp % 4, 1, :]
                    if phase == 0:
                        wait_apart(pool, pool_passed, att["y_rstd"], p + 1)
                        nc.gpsimd.tensor_scalar(zn, z, mv[:, 0:1], rs[:, 1:2], ALU.subtract, ALU.mult).then_inc(att["y_ready"], 1)
                    else:
                        if kp >= NT + 4:
                            pool.wait_ge(att["tok_done"], p - 3 - NT)
                            pool.wait_ge(moe["tok_kept"], p - 3 - NT)
                        q = p - NT
                        wait_apart(pool, pool_passed, att["y_rstd"], p + 1)
                        nc.gpsimd.tensor_scalar(zn, z, mv[:, 0:1], rs[:, 1:2], ALU.subtract, ALU.mult).then_inc(att["y_norm"], 1)
                        pool.wait_ge(att["y_norm"], q + 1)
                        nc.gpsimd.tensor_tensor(z, zn, ln1[:, 0, :], ALU.mult).then_inc(att["y_gain"], 1)
                        pool.wait_ge(att["y_gain"], q + 1)
                        nc.gpsimd.tensor_tensor(zn, z, ln1[:, 1, :], ALU.add).then_inc(att["y_ready"], 1)

                q, kq = t_ - 12 - NT, k - 12 - NT
                if phase == 1 and (looping or 0 <= kq < NT):
                    wait_apart(pool, pool_passed, moe["tok_copied"], 2 * q + 2)
                    wait_apart(pool, pool_passed, moe["idx_copied"], q + 1)
                    for c in range(TOP):
                        nc.gpsimd.indirect_dma_start(
                            out=packed, out_offset=bass.IndirectOffsetOnAxis(ap=idx_slot[:, kq % 4, c:c + 1], axis=0),
                            in_=tok_slot[:, kq % 4, c, :], in_offset=None).then_inc(packed_out[kq % 4], 16)

            run_attention(pool, 0, step)
            run_attention(pool, 1, step)


            def expert_step(t_, k, looping):
                p, kp = t_ - 2, k - 2
                if looping or 0 <= kp < NM:
                    wait_apart(pool, pool_passed, moe["place_ready"], p + 1)
                    wait_apart(pool, pool_passed, moe["yo_ready"], p + 1)
                    nc.gpsimd.indirect_dma_start(
                        out=results, out_offset=bass.IndirectOffsetOnAxis(ap=xs_place[:, kp % 4, :], axis=0),
                        in_=y_sb[:, kp % 4, :], in_offset=None).then_inc(y_out[kp % 4], 16)

            run_tiles(pool, NM, 2, 3, expert_step)

            for g in range(NT // COMBINE):
                rs = rs_z[:, g % 2, :, :]
                pool.wait_ge(moe["z_mv"], COMBINE * (g + 1))
                if g >= 2:
                    pool.wait_ge(moe["z_norm"], COMBINE * (g - 1))
                nc.gpsimd.tensor_scalar(rs[:, :, 0:1], mv_z[:, g % 2, :, 1:2], EPS, None, ALU.add).then_inc(moe["z_var"], 1)
                pool.wait_ge(moe["z_var"], g + 1)
                nc.gpsimd.tensor_tensor(rs[:, :, 1:2], rs[:, :, 0:1], neg_half[:, :].unsqueeze(1).broadcast_to([P, COMBINE, 1]), ALU.pow).then_inc(moe["z_rstd"], 1)
                if g >= 1:
                    z = x_all[:, (g - 1) * COMBINE:g * COMBINE, :]
                    pool.wait_ge(moe["z_norm"], COMBINE * g)
                    nc.gpsimd.tensor_tensor(z, z, ln2[:, 0:1, :].broadcast_to([P, COMBINE, D]), ALU.mult).then_inc(moe["z_gain"], 1)
                    pool.wait_ge(moe["z_gain"], g)
                    pool.wait_ge(moe["x1_added"], 4)
                    nc.gpsimd.tensor_tensor(z, z, src_all[:, (g - 1) * COMBINE:g * COMBINE, :], ALU.add).then_inc(moe["o_done"], 1)

        @block.vector
        def _(dve):
            nc.vector.memset(zero_tile[:, :], 0.0).then_inc(zero_ready, 1)
            dve.wait_ge(const_in, 16 * CONSTANTS)
            nc.vector.memset(neg_half[:, :], -0.5).then_inc(prep, 1)
            nc.vector.memset(ones[:, :], 1.0).then_inc(zero_ready, 1)
            nc.vector.tensor_copy(earlier_b[:, :], earlier[:, :]).then_inc(zero_ready, 1)
            nc.vector.tensor_scalar(decay[:, :], dist[:, :], td[:, :], -ROOT, ALU.mult, ALU.mult).then_inc(prep, 1)
            nc.vector.tensor_copy(bias_v_wide[:, :, :], bias_v[:, :].unsqueeze(2).broadcast_to([P, 2, P])).then_inc(row_done, 1)
            dve.wait_ge(row_done, 2)
            nc.vector.tensor_tensor(row_add[:, :, :], ps_o[:, 0:2 * D].rearrange("p (a b) -> p a b", a=2), bias_o[:, :, :], ALU.add).then_inc(row_ready, 1)
            dve.wait_ge(prep, 2)
            dve.wait_ge(x_in0, 16)

            v = nc.vector
            by_expert = rank8[:, :].unsqueeze(1).broadcast_to([P, 4, N_EXP])

            def across(a):
                return a.unsqueeze(2).broadcast_to([P, 4, N_EXP])

            def after(q, lines):
                dve.wait_ge(moe["route"], q * (ROUTE // 4) + lines)

            def after_apart(q, lines):
                wait_apart(dve, dve_passed, moe["route"], q * (ROUTE // 4) + lines)

            def route_choice(c, n, q):
                g = bass.ds(q, 4)
                left, key = rest if c else logit, r_key[:, 0, g, :]
                done = 6 * c + n
                if n == 0:
                    if c == 0:
                        wait_apart(dve, dve_passed, att["logits_read"], q + 4)
                    else:
                        after_apart(q, done)
                    line = v.tensor_reduce(best[:, c, g], left[:, g, :], AX.X, ALU.max)
                elif n == 1:
                    after(q, done)
                    line = v.tensor_tensor(key, left[:, g, :], across(best[:, c, g]), ALU.is_equal)
                elif n == 2:
                    after(q, done)
                    line = v.tensor_tensor(key, key, by_expert, ALU.mult)
                elif n == 3:
                    after_apart(q, done)
                    line = v.tensor_reduce(r_top[:, g], key, AX.X, ALU.max)
                elif n == 4:
                    after(q, done)
                    line = v.tensor_tensor(pick[:, c, g, :], by_expert, across(r_top[:, g]), ALU.is_equal)
                elif c == 0:
                    after(q, done)
                    line = v.scalar_tensor_tensor(out=rest[:, g, :], in0=pick[:, 0, g, :], scalar=-FAR, in1=logit[:, g, :], op0=ALU.mult, op1=ALU.add)
                else:
                    after(q, done)
                    line = v.tensor_tensor(both[:, g, :], pick[:, 0, g, :], pick[:, 1, g, :], ALU.add)
                line.then_inc(moe["route"], 1)

            def route_rows(q):
                after(q, 12)
                dve.wait_ge(moe["counted"], q + 4)
                v.tensor_tensor(place[:, bass.ds(q, 4), :], ps_y[:, 256:256 + 4 * N_EXP].rearrange("p (t e) -> p t e", t=4),
                                running[:, :].unsqueeze(1).broadcast_to([P, 4, N_EXP]), ALU.add).then_inc(moe["route"], 1)
                after(q, 13)
                v.tensor_tensor(running[:, :], running[:, :], ps_y[:, 288:288 + N_EXP], ALU.add).then_inc(moe["route"], 1)

            def route_slots(n, q):
                g, c = bass.ds(q, 4), n % TOP
                if n < 2:
                    after(q, 14)
                    line = v.tensor_tensor(r_key[:, c, g, :], place[:, g, :], pick[:, c, g, :], ALU.mult)
                elif n < 4:
                    after_apart(q, 14 + n - 1)
                    line = v.tensor_reduce(slot_f[:, c, g], r_key[:, c, g, :], AX.X, ALU.add)
                else:
                    after_apart(q, 14 + n - 1)
                    line = v.tensor_copy(slot_u[:, c, g], slot_f[:, c, g])
                line.then_inc(moe["route"], 1)

            def routing(late, n, t_, k, phase, looping):
                behind = {1: 9, 2: 10, 0: 12}.get(k % 4)
                if phase == 1 and behind and late == (k % 4 == 1) and (looping or 0 <= k - behind - NT < NT):
                    q = t_ - behind - NT
                    if k % 4 == 0:
                        route_slots(n, q)
                    else:
                        route_choice(k % 4 - 1, n, q)

            def step(t_, k, phase, looping):
                p, kp = t_, k
                here = live(kp, phase, looping)
                sc = ps_s[:, :].rearrange("p (h k) -> p h k", h=H)
                high = neg_max[:, kp % 2, :]
                a = prob[:, kp % 2, :, :]
                if here:
                    dve.wait_ge(att["scores_done"], p + 1)
                    if kp >= 2:
                        dve.wait_ge(att["pt_done"], p - 1)
                        dve.wait_ge(att["shifted"], p - 1)
                    if phase == 0:
                        nc.vector.tensor_tensor(a, sc, decay[:, :].unsqueeze(1).broadcast_to([P, H, S]), ALU.add).then_inc(att["scores_read"], 1)
                    else:
                        nc.vector.tensor_reduce(high, sc, AX.X, ALU.max, negate=True).then_inc(att["max_ready"], 1)
                routing(False, 0, t_, k, phase, looping)
                p2, k2 = t_ - 2, k - 2
                if live(k2, phase, looping):
                    o = ps_o[:, 0:H * (DH + 1)].rearrange("p (h c) -> p h c", h=H)
                    dve.wait_ge(att["pv_done"], p2 + 1)
                    nc.vector.reciprocal(inv_sum[:, k2 % 2, :].unsqueeze(2), o[:, :, DH:DH + 1]).then_inc(att["inv_ready"], 1)
                routing(False, 1, t_, k, phase, looping)
                if here:
                    if phase == 0:
                        dve.wait_ge(att["scores_read"], p + 1)
                        nc.vector.tensor_reduce(high, a, AX.X, ALU.max, negate=True).then_inc(att["max_ready"], 1)
                    else:
                        dve.wait_ge(att["max_ready"], p + 1)
                        nc.vector.tensor_tensor(a, sc, high.unsqueeze(2).broadcast_to([P, H, S]), ALU.add).then_inc(att["shifted"], 1)
                routing(False, 2, t_, k, phase, looping)
                if live(k2, phase, looping):
                    dve.wait_ge(att["inv_ready"], p2 + 1)
                    if k2 >= 2:
                        dve.wait_ge(att["ot_done"], p2 - 1)
                    nc.vector.tensor_tensor(o_sb[:, k2 % 2, :].rearrange("p (h d) -> p h d", h=H), o[:, :, 0:DH],
                                            inv_sum[:, k2 % 2, :].unsqueeze(2).broadcast_to([P, H, DH]), ALU.mult).then_inc(att["o_ready"], 1)
                p, kp = t_ - 6, k - 6
                if phase == 1 and live(kp, phase, looping):
                    q = p - NT
                    dve.wait_ge(att["logits_done"], q + 1)
                    nc.vector.tensor_tensor(logit[:, q, :], ps_o[:, 256:256 + N_EXP], bias_g[:, :], ALU.add).then_inc(att["logits_read"], 1)
                routing(True, 0, t_, k, phase, looping)
                routing(False, 3, t_, k, phase, looping)
                p, kp = t_ + 2, k + 2
                if live(kp, phase, looping):
                    dve.wait_ge(att["proj_done"], p + 1)
                    if kp >= 2:
                        dve.wait_ge(att["scores_done"], p - 1)
                    for n, (dst, mask) in enumerate(((qm, mask_q), (kx, mask_k))):
                        nc.vector.scalar_tensor_tensor(
                            out=dst[:, kp % 2, :, :], in0=ps_qk[:, n * P:n * P + P].unsqueeze(1).broadcast_to([P, G4, P]),
                            scalar=bias_qk[:, phase, n:n + 1], in1=mask[:, :].unsqueeze(2).broadcast_to([P, G4, P]),
                            op0=ALU.add, op1=ALU.mult).then_inc(att["qk_ready"], 1)
                        if n == 0:
                            routing(True, 1, t_, k, phase, looping)
                            routing(False, 4, t_, k, phase, looping)
                else:
                    routing(True, 1, t_, k, phase, looping)
                    routing(False, 4, t_, k, phase, looping)
                routing(True, 2, t_, k, phase, looping)
                routing(False, 5, t_, k, phase, looping)
                p, kp = t_ + 4, k + 4
                rows_in = phase == 0 and live(kp, phase, looping)
                if rows_in:
                    if kp == 8:
                        dve.wait_ge(x_in1, 16)
                    if kp >= 2:
                        dve.wait_ge(att["xn_ready"], p - 1)
                    nc.vector.bn_stats(stats_a[:, kp % 2, :], x_all[:, p, :]).then_inc(att["x_stats"], 1)
                p2, k2 = t_ - 3, k - 3
                rows_out = live(k2, phase, looping)
                if rows_out:
                    dve.wait_ge(att["y_done"], p2 + 1)
                if phase == 1 and k % 4 == 3 and (looping or 0 <= k - 11 - NT < NT):
                    route_rows(t_ - 11 - NT)
                if rows_out:
                    dve.wait_ge(att["residual_ready"], p2 + 1)
                    if phase == 0:
                        if k2 >= 4:
                            dve.wait_ge(stored[k2 % 4], 4 * (p2 - k2 % 4))
                    else:
                        dve.wait_ge(att["y_ready"], p2 - 3)
                        dve.wait_ge(stored[k2 % 4], 16 * NT // 4)
                    z = res[:, k2 % 4, 0, :]
                    nc.vector.tensor_tensor(z, ps_y[:, P:2 * P], (x_all, src_all)[phase][:, p2 - phase * NT, :], ALU.add).then_inc(att["y_read"], 1)
                routing(True, 3, t_, k, phase, looping)
                if rows_in:
                    wait_apart(dve, dve_passed, att["x_stats"], p + 1)
                    nc.vector.bn_aggr(mv_a[:, kp % 2, :], stats_a[:, kp % 2, :]).then_inc(att["x_mv"], 1)
                if rows_out:
                    dve.wait_ge(att["y_read"], p2 + 1)
                    if k2 >= 2:
                        dve.wait_ge(att["y_ready"], p2 - 1)
                    nc.vector.bn_stats(stats_b[:, k2 % 2, :], z).then_inc(att["y_stats"], 1)
                routing(True, 4, t_, k, phase, looping)
                if rows_out:
                    wait_apart(dve, dve_passed, att["y_stats"], p2 + 1)
                    nc.vector.bn_aggr(mv_b[:, k2 % 2, :], stats_b[:, k2 % 2, :]).then_inc(att["y_mv"], 1)
                routing(True, 5, t_, k, phase, looping)
                p3, k3 = t_ - 3, k - 3
                if phase == 0 and live(k3, phase, looping):
                    dve.wait_ge(moe["w_hi_ready"], p3 + 1)
                    chunks = bass.ds(p3 * (W_PART // P), W_PART // P)
                    nc.vector.tensor_tensor(w_split[:, chunks, 1, :], w_given[:, bass.ds(p3 * W_PART, W_PART)].rearrange("p (c f) -> p c f", f=P),
                                            w_split[:, chunks, 0, :].bitcast(FP32), ALU.subtract).then_inc(moe["w_lo_ready"], 1)
                if rows_in:
                    dve.wait_ge(att["x_rstd"], p + 1)
                    if kp >= 2:
                        dve.wait_ge(att["in_done"], p - 1)
                    nc.vector.tensor_scalar(xn[:, kp % 2, :], x_all[:, p, :], mv_a[:, kp % 2, 0:1], rs_a[:, kp % 2, 1:2],
                                            ALU.subtract, ALU.mult).then_inc(att["xn_ready"], 1)

            run_attention(dve, 0, step)
            dve.wait_ge(moe["w_lo_ready"], NT)
            v.tensor_copy(running[:, :], region_at[:, :]).then_inc(prep, 1)
            dve.wait_ge(prep, 3)
            run_attention(dve, 1, step)

            made = [ROUTE * NT // 4]

            def then(instruction):
                made[0] += 1
                instruction.then_inc(moe["route"], 1)
                dve.wait_ge(moe["route"], made[0])

            dve.wait_ge(moe["route"], made[0])
            v.tensor_tensor(r_sum[:, :], best[:, 1, :], best[:, 0, :], ALU.subtract).then_inc(moe["route_exp"], 1)
            then(v.tensor_copy(ends[:, :], running[:, :]))
            then(v.tensor_tensor(filled[:, :], running[:, :], region_at[:, :], ALU.subtract))
            then(v.tensor_tensor(full[:, :, :], filled[:, :].unsqueeze(2).broadcast_to([P, N_EXP, NT]),
                                 steps128[:, :].unsqueeze(1).broadcast_to([P, N_EXP, NT]), ALU.is_gt))
            then(v.tensor_reduce(tiles_of[:, :], full[:, :, :], AX.X, ALU.add))
            then(v.tensor_copy(tiles_to[:, 0, :], tiles_of[:, :]))
            at, gap = 0, 1
            while gap < N_EXP:
                then(v.tensor_copy(tiles_to[:, 1 - at, 0:gap], tiles_to[:, at, 0:gap]))
                then(v.tensor_tensor(tiles_to[:, 1 - at, gap:], tiles_to[:, at, gap:], tiles_to[:, at, 0:N_EXP - gap], ALU.add))
                at, gap = 1 - at, 2 * gap
            then(v.tensor_tensor(past[:, :, :], tile_no[:, :].unsqueeze(2).broadcast_to([P, NM, N_EXP]),
                                 tiles_to[:, at, :].unsqueeze(1).broadcast_to([P, NM, N_EXP]), ALU.is_ge))
            then(v.tensor_reduce(expert_f[:, :], past[:, :, 0:N_EXP - 1], AX.X, ALU.add))
            then(v.tensor_copy(expert_of[:, :], expert_f[:, :]))
            then(v.tensor_scalar(filled[:, :], tiles_of[:, :], float(-P), float(REGION), ALU.mult, ALU.add))
            then(v.tensor_tensor(past[:, :, :], past[:, :, :], filled[:, :].unsqueeze(1).broadcast_to([P, NM, N_EXP]), ALU.mult))
            then(v.tensor_reduce(row_f[:, :], past[:, :, :], AX.X, ALU.add))
            then(v.scalar_tensor_tensor(out=row_f[:, :], in0=tile_no[:, :], scalar=float(P), in1=row_f[:, :], op0=ALU.mult, op1=ALU.add))
            v.tensor_copy(row_of[:, :], row_f[:, :]).then_inc(moe["tiles_known"], 1)
            dve.wait_ge(moe["tiles_known"], 1)
            dve.wait_ge(moe["route_exp"], 2)
            then(v.tensor_scalar(r_sum[:, :], r_exp[:, :], 1.0, None, ALU.add))
            then(v.reciprocal(share[:, 0, :], r_sum[:, :]))
            then(v.tensor_tensor(share[:, 1, :], share[:, 0, :], r_exp[:, :], ALU.mult))
            dve.wait_ge(const2_in, 16 * (NT + 1))
            for n in range(4):
                dve.wait_ge(x1_read[n], 32)
                x1 = src_all[:, 8 * n:8 * n + 8, :]
                v.tensor_tensor(x1, x1, ln2[:, 1:2, :].broadcast_to([P, 8, D]), ALU.add).then_inc(moe["x1_added"], 1)

            experts = {}

            def expert_step(t_, k, looping):
                load_experts(mybir.EngineType.DVE, t_, k, looping, experts)
                p, kp = t_ + 1, k + 1
                if looping or 0 <= kp < NM:
                    dve.wait_ge(moe["xhi_ready"], p + 1)
                    v.tensor_tensor(x_lo[:, kp % 2, :], ps_in[:, 0:P], x_hi[:, kp % 2, :].bitcast(FP32), ALU.subtract).then_inc(moe["xlo_ready"], 1)
                p, kp = t_, k
                if looping or 0 <= kp < NM:
                    e = experts[kp]
                    dve.wait_ge(moe["h_done"], p + 1)
                    if kp >= 2:
                        dve.wait_ge(moe["ht_done"], p - 1)
                    v.tensor_tensor(h_sb[:, kp % 2, :], ps_s[:, F * (kp % 2):F * (kp % 2 + 1)], b1_wide[:, e, :], ALU.add).then_inc(moe["hb_ready"], 1)
                p, kp = t_ - 1, k - 1
                if looping or 0 <= kp < NM:
                    dve.wait_ge(moe["hhi_ready"], p + 1)
                    v.scalar_tensor_tensor(out=h_lo[:, kp % 2, :], in0=ps_pt[:, F * (kp % 2):F * (kp % 2 + 1)], scalar=0.0,
                                           in1=h_hi[:, kp % 2, :].bitcast(FP32), op0=ALU.max, op1=ALU.subtract).then_inc(moe["hlo_ready"], 1)
                p2, k2 = t_ - 2, k - 2
                results_here = looping or 0 <= k2 < NM
                if results_here:
                    y, a = y_sb[:, k2 % 4, :], (ps_o, ps_y)[k2 % 2]
                    dve.wait_ge(moe["yy_done"], p2 + 1)
                    if k2 >= 4:
                        dve.wait_ge(y_out[k2 % 4], 4 * (p2 - k2 % 4))
                    v.tensor_tensor(y, a[:, 0:D], b2_wide[:, experts[k2], :], ALU.add).then_inc(moe["yb_ready"], 1)
                p, kp = t_, k
                if looping or 0 <= kp < NM:
                    dve.wait_ge(xs_in[kp % 4], 4 * (p - kp % 4) + 16)
                    if kp >= 4:
                        dve.wait_ge(y_out[kp % 4], 4 * (p - kp % 4))
                    v.tensor_tensor(xs_place[:, kp % 4, :], xs[:, kp % 4, D:D + 1], padding_at[:, bass.ds(p, 1)], ALU.max).then_inc(moe["place_ready"], 1)
                if results_here:
                    dve.wait_ge(moe["yb_ready"], p2 + 1)
                    v.tensor_tensor(y, a[:, D:2 * D], y, ALU.add).then_inc(moe["yo_ready"], 1)

            run_tiles(dve, NM, 2, 3, expert_step)

            def shift(g):
                rs = rs_z[:, g % 2, :, :]
                dve.wait_ge(moe["z_rstd"], g + 1)
                v.scalar_tensor_tensor(out=rs[:, :, 2:3], in0=mv_z[:, g % 2, :, 0:1], scalar=-1.0, in1=rs[:, :, 1:2],
                                       op0=ALU.mult, op1=ALU.mult).then_inc(moe["z_shift"], 1)

            for g in range(NT // COMBINE):
                tiles = range(g * COMBINE, (g + 1) * COMBINE)
                dve.wait_ge(got_in[g % 4], 2 * 16 * (g // 4 + 1))
                for p in tiles:
                    v.scalar_tensor_tensor(out=x_all[:, p, :], in0=got[g % 4][:, 0, p % COMBINE, :], scalar=share[:, 0, p:p + 1], in1=x_all[:, p, :],
                                           op0=ALU.mult, op1=ALU.add).then_inc(moe["z_part"], 1)
                if g >= 1:
                    shift(g - 1)
                for p in tiles:
                    dve.wait_ge(moe["z_part"], p + 1)
                    v.scalar_tensor_tensor(out=x_all[:, p, :], in0=got[g % 4][:, 1, p % COMBINE, :], scalar=share[:, 1, p:p + 1], in1=x_all[:, p, :],
                                           op0=ALU.mult, op1=ALU.add).then_inc(moe["z_ready"], 1)
                for p in tiles:
                    dve.wait_ge(moe["z_ready"], p + 1)
                    v.bn_stats(stats_z[:, g % 2, p % COMBINE, :], x_all[:, p, :]).then_inc(moe["z_stats"], 1)
                for p in tiles:
                    dve.wait_ge(moe["z_stats"], p + 1)
                    v.bn_aggr(mv_z[:, g % 2, p % COMBINE, :], stats_z[:, g % 2, p % COMBINE, :]).then_inc(moe["z_mv"], 1)
            shift(NT // COMBINE - 1)
            z = x_all[:, NT - COMBINE:NT, :]
            dve.wait_ge(moe["z_norm"], NT)
            v.tensor_tensor(z, z, ln2[:, 0:1, :].broadcast_to([P, COMBINE, D]), ALU.mult).then_inc(moe["last_gain"], 1)
            dve.wait_ge(moe["last_gain"], 1)
            v.tensor_tensor(z, z, src_all[:, NT - COMBINE:NT, :], ALU.add).then_inc(moe["last_done"], 1)

        @block.tensor
        def _(pe):
            pe.wait_ge(const_in, 16 * CONSTANTS)
            pe.wait_ge(zero_ready, 3)
            pe.wait_ge(weights_in, 16)
            pe.wait_ge(row_done, 1)
            for n in range(2):
                m = nc.tensor.matmul(ps_o[:, n * D:(n + 1) * D], bias_v_wide[:, n, :], w_t[:, 4 * n + 3, :], start=True, stop=True)
            m.then_inc(row_done, 1)

            def step(t_, k, phase, looping):
                p, kp = t_, k
                if live(kp, phase, looping):
                    pe.wait_ge(att["qk_ready"], 2 * p + 2)
                    if kp >= 1:
                        pe.wait_ge(att["shifted"] if phase else att["scores_read"], p)
                    for g in range(G4):
                        for b in range(2):
                            q = slice(64 * b, 64 * b + 64)
                            m = nc.tensor.matmul(ps_s[q, 256 * g:256 * g + 256], qm[:, kp % 2, g, q], kx[:, kp % 2, :, q], start=True, stop=True)
                    m.then_inc(att["scores_done"], 1)
                p, kp = t_ - 5, k - 5
                if phase == 1 and live(kp, phase, looping):
                    pe.wait_ge(att["y_ready"], p + 1)
                    if kp >= NT + 1:
                        pe.wait_ge(att["tok_ready"], p - NT)
                    pe.wait_ge(att["in_ready"], t_ + 3 if looping or k + 2 < 2 * NT else 2 * NT)
                    pe.wait_ge(att["v_ready"], 2 * t_ + 4 if looping or k + 1 < 2 * NT else 4 * NT)
                    nc.tensor.transpose(ps_in[:, 0:P], res[:, kp % 4, 1, :], ident[:, :]).then_inc(att["tok_done"], 1)
                p, kp = t_ - 6, k - 6
                if phase == 1 and live(kp, phase, looping):
                    pe.wait_ge(att["tok_ready"], p + 1 - NT)
                    pe.wait_ge(att["o_ready"], t_ - 2 if looping or k - 3 < 2 * NT else 2 * NT)
                    if kp >= NT + 1:
                        pe.wait_ge(att["logits_read"], p - NT)
                    nc.tensor.matmul(ps_o[:, 256:256 + N_EXP], tok_t[:, kp % 2, :], gate_t[:, :], start=True, stop=True).then_inc(att["logits_done"], 1)
                p, kp = t_ - 2, k - 2
                if live(kp, phase, looping):
                    pe.wait_ge(att["pt_ready"], p + 1)
                    pe.wait_ge(att["v_ready"], 2 * p + 2)
                    if kp >= 1:
                        pe.wait_ge(att["o_ready"], p)
                    if phase == 1 and kp >= NT + 5:
                        pe.wait_ge(att["logits_read"], p - 4 - NT)
                    for h in range(H // 2):
                        for b in range(2):
                            m = nc.tensor.matmul(ps_o[64 * b:64 * b + 64, h * VW:(h + 1) * VW], probt[:, kp % 2, h, 64 * b:64 * b + 64],
                                                 vb[:, kp % 4, b, h, :, :], start=True, stop=True)
                    m.then_inc(att["pv_done"], 1)
                p, kp = t_ + 2, k + 2
                if live(kp, phase, looping):
                    pe.wait_ge(att["in_ready"], p + 1)
                    if kp >= 1:
                        pe.wait_ge(att["qk_ready"], 2 * p)
                        pe.wait_ge(att["v_ready"], 2 * p)
                    if phase == 1 and k - 5 >= NT:
                        pe.wait_ge(att["tok_ready"], t_ - 4 - NT)
                    xt, ct = xct[:, kp % 2, 0, :], xct[:, kp % 2, 1 - phase, :]
                    w = 4 * phase
                    nc.tensor.matmul(ps_qk[:, 0:P], w_t[:, w, :], xt, start=True, stop=True)
                    nc.tensor.matmul(ps_qk[:, P:2 * P], w_t[:, w + 1, :], ct, start=True, stop=True)
                    for b in range(2):
                        for par in range(2):
                            m = nc.tensor.matmul(ps_in[64 * par:64 * par + 64, 256 + P * b:256 + P * b + P], ct[:, 64 * b:64 * b + 64], w_t[:, w + 2, :], start=True, stop=True)
                    m.then_inc(att["proj_done"], 1)
                q, kq = t_ - 11 - NT, k - 11 - NT
                if phase == 1 and k % 4 == 3 and (looping or 0 <= kq < NT):
                    pe.wait_ge(moe["route"], q * (ROUTE // 4) + 12)
                    pe.wait_ge(att["y_read"], t_ - 3 if looping or k - 4 < 2 * NT else 2 * NT)
                    ranks = ps_y[:, 256:256 + 4 * N_EXP].rearrange("p (t e) -> p t e", t=4)
                    nc.tensor.matmul(ranks, earlier_b[:, :], both[:, bass.ds(q, 4), :], start=True, stop=False)
                    for n in range(3):
                        nc.tensor.matmul(ranks[:, n + 1:, :], ones[:, :], both[:, bass.ds(q + n, 1), :].broadcast_to([P, 3 - n, N_EXP]), start=False, stop=n == 2)
                    for n in range(4):
                        m = nc.tensor.matmul(ps_y[:, 288:288 + N_EXP], ones[:, :], both[:, q + n, :], start=n == 0, stop=n == 3)
                    m.then_inc(moe["counted"], 4)
                p, kp = t_ - 3, k - 3
                if live(kp, phase, looping):
                    pe.wait_ge(att["o_ready"], p + 1)
                    if kp >= 1:
                        pe.wait_ge(att["y_read"], p)
                    nc.tensor.transpose(ps_y[:, 0:P], o_sb[:, kp % 2, :], ident[:, :]).then_inc(att["ot_done"], 1)
                p, kp = t_ - 1, k - 1
                if live(kp, phase, looping):
                    pe.wait_ge(att["probs_ready"], p + 1)
                    if kp >= 1:
                        pe.wait_ge(att["pt_ready"], p)
                    for h in range(H // 2):
                        m = nc.tensor.transpose(ps_pt[:, h * P:(h + 1) * P], prob[:, kp % 2, 2 * h:2 * h + 2, :], ident[:, :])
                    m.then_inc(att["pt_done"], 1)
                p, kp = t_ + 3, k + 3
                if live(kp, phase, looping):
                    pe.wait_ge(att["xn_ready"], p + 1)
                    if kp >= 1:
                        pe.wait_ge(att["v_ready"], 2 * p)
                        pe.wait_ge(att["in_ready"], p)
                    if phase == 0:
                        pe.wait_ge(ctx_ready[kp % 4], 4 * (p - kp % 4) + 16)
                        nc.tensor.transpose(ps_in[:, P:2 * P], ctx_in[:, kp % 4, :], ident[:, :])
                    nc.tensor.transpose(ps_in[:, 0:P], xn[:, kp % 2, :], ident[:, :]).then_inc(att["in_done"], 1)
                p, kp = t_ - 3, k - 3
                if live(kp, phase, looping):
                    pe.wait_ge(att["ot_ready"], p + 1)
                    nc.tensor.matmul(ps_y[:, P:2 * P], ot_sb[:, kp % 2, :], w_t[:, 4 * phase + 3, :], start=True, stop=True).then_inc(att["y_done"], 1)

            run_attention(pe, 0, step)
            run_attention(pe, 1, step)

            pe.wait_ge(moe["tiles_known"], 1)
            experts = {}

            def expert_step(t_, k, looping):
                load_experts(mybir.EngineType.PE, t_, k, looping, experts)
                p, kp = t_ + 1, k + 1
                if looping or 0 <= kp < NM:
                    pe.wait_ge(xs_in[kp % 4], 4 * (p - kp % 4) + 16)
                    if kp >= 1:
                        pe.wait_ge(moe["xlo_ready"], p)
                    nc.tensor.transpose(ps_in[:, 0:P], xs[:, kp % 4, 0:D], ident[:, :]).then_inc(moe["xt_done"], 1)
                p, kp = t_, k
                if looping or 0 <= kp < NM:
                    e = experts[kp]
                    pe.wait_ge(moe["xlo_ready"], p + 1)
                    if kp >= 2:
                        pe.wait_ge(moe["hb_ready"], p - 1)
                    a = ps_s[:, F * (kp % 2):F * (kp % 2 + 1)]
                    nc.tensor.matmul(a, x_lo[:, kp % 2, :], w1_split[:, e, :, 0, :], start=True, stop=False)
                    nc.tensor.matmul(a, x_hi[:, kp % 2, :], w1_split[:, e, :, 1, :], start=False, stop=False)
                    nc.tensor.matmul(a, x_hi[:, kp % 2, :], w1_split[:, e, :, 0, :], start=False, stop=True).then_inc(moe["h_done"], 1)
                p, kp = t_ - 1, k - 1
                if looping or 0 <= kp < NM:
                    pe.wait_ge(moe["hb_ready"], p + 1)
                    if kp >= 2:
                        pe.wait_ge(moe["hlo_ready"], p - 1)
                    for c in range(FC):
                        m = nc.tensor.transpose(ps_pt[:, F * (kp % 2) + c * P:F * (kp % 2) + (c + 1) * P], h_sb[:, kp % 2, c * P:(c + 1) * P], ident[:, :])
                    m.then_inc(moe["ht_done"], 1)
                p, kp = t_ - 2, k - 2
                if looping or 0 <= kp < NM:
                    e = experts[kp]
                    pe.wait_ge(moe["hlo_ready"], p + 1)
                    if kp >= 2:
                        pe.wait_ge(moe["yo_ready"], p - 1)
                    a = (ps_o, ps_y)[kp % 2]
                    for c in range(FC):
                        chunk = slice(c * P, (c + 1) * P)
                        if c == FC - 1:
                            for b in range(FC):
                                nc.tensor.matmul(a[:, 0:D], h_lo[:, kp % 2, b * P:(b + 1) * P], w2_split[:, e, b, 0, :], start=False, stop=False)
                        m = nc.tensor.matmul(a[:, 0:2 * D], h_hi[:, kp % 2, chunk], w2_split[:, e, c, :, :], start=c == 0, stop=c == FC - 1)
                    m.then_inc(moe["yy_done"], 1)

            run_tiles(pe, NM, 2, 3, expert_step)


_SHORT = {"x": "x", "ctx_1024": "ctx"}


def kernel(**inputs):
    import numpy as _np
    import concourse.bacc as _bacc
    from concourse import mybir as _mybir
    from concourse.bass_utils import run_bass_kernel_spmd as _run

    nc = _bacc.Bacc("TRN2", target_bir_lowering=False, num_devices=1)
    arrays, t = {}, {}
    part = _np.arange(P)
    columns = (
        _np.eye(P), _np.abs(part[:, None] % S - _np.arange(S)), part[:, None] // 32 == _np.arange(G4),
        part[:, None] // DH % G4 == _np.arange(G4), part[:, None] < part, _np.tile(N_EXP - _np.arange(N_EXP), (P, 1)), _np.tile(_np.arange(N_EXP) * REGION, (P, 1)),
        _np.tile(_np.arange(NT) * P, (P, 1)), _np.tile(_np.arange(NM), (P, 1)),
        part[:, None] + (NM + _np.arange(TOP * NT)) * P, part[:, None] + _np.arange(NM) * P)
    given = {_SHORT.get(n, n.replace("L0_xattn_", "").replace("L0_ffn_", "")): _np.asarray(a) for n, a in inputs.items()}
    in_b = given["in_proj_b"]
    laid = {
        "shapes": _np.concatenate(columns, axis=1, dtype=_np.float32),
        "weights": _np.stack([given[n].T for n in ("wq", "wk", "wv", "wo")] + [a.T for a in given["in_proj_w"].reshape(3, D, D)] + [given["out_w"].T], axis=1),
        "gate_w": given["gate_w"].T,
        "expert_w": _np.concatenate([given["w1"].transpose(2, 0, 1).reshape(P, N_EXP * F),
                                     given["w2"].reshape(N_EXP, D, FC, P).transpose(3, 0, 2, 1).reshape(P, N_EXP * F)], axis=1),
        "columns": _np.stack([given["bq"], given["bk"], in_b[0:D], in_b[D:2 * D], given["bv"], in_b[2 * D:]], axis=1),
        "rows": _np.stack([given[n] for n in ("bo", "out_b", "ln1_g", "ln1_b", "ln2_g", "ln2_b")]),
        "time_decay": given["time_decay"].reshape(1, 1),
    }
    for name in ("x", "ctx", "gate_b", "b1", "b2"):
        laid[name] = given[name]
    for name, a in laid.items():
        a = _np.ascontiguousarray(a)
        arrays[f"in_{name}"] = a
        t[name] = nc.dram_tensor(f"in_{name}", a.shape, _mybir.dt.from_np(a.dtype), kind="ExternalInput").ap()
    out = nc.dram_tensor("out_0", (B, S, D), FP32, kind="ExternalOutput").ap()
    scratch = nc.dram_tensor("scratch", (B * S, 2, D), FP32).ap()
    packed = nc.dram_tensor("packed", (N_EXP * REGION + SPARE * P, D + 1), FP32).ap()
    results = nc.dram_tensor("results", ((NM + TOP * NT) * P, D), FP32).ap()
    build(nc, t, out, scratch, packed, results)
    r = _run(nc, [arrays], core_ids=[0])
    return r.results[0]["out_0"]
```
